# Optimizing a Trainium2 kernel written in Bass

```python
import numpy as np
import jax
import jax.numpy as jnp

def _softmax(x, axis=-1):
    return jax.nn.softmax(x, axis=axis)

def _gelu(x):
    return jax.nn.gelu(x, approximate=True)

def _silu(x):
    return jax.nn.silu(x)

def _sigmoid(x):
    return jax.nn.sigmoid(x)

def _layernorm(x, axis=-1, eps=1e-05):
    m = jnp.mean(x, axis=axis, keepdims=True)
    v = jnp.var(x, axis=axis, keepdims=True)
    return (x - m) / jnp.sqrt(v + eps)

def _scatter_add(tgt, idx, src, axis=0):
    return tgt.at[idx].add(src)

def _segment_sum(src, seg, n):
    return jax.ops.segment_sum(src, seg, n)
kernel_name = 'mk_prb_d1_jaxref_r8_1e1753'

def setup_inputs(seed: int=0):
    np.random.seed(seed)
    _w = jnp.asarray

    def _L0_attn_setup():
        import jax, jax.numpy as jnp
        import numpy as np
        L, D, F, H = (4, 128, 256, 8)
        DH = D // H
        EPS = 1e-05

        def _layer_norm(x, scale, bias):
            mu = x.mean(-1, keepdims=True)
            var = x.var(-1, keepdims=True)
            return (x - mu) * jax.lax.rsqrt(var + EPS) * scale + bias

        def _rotate(x, cos, sin):
            x1, x2 = (x[..., 0::2], x[..., 1::2])
            r1 = x1 * cos - x2 * sin
            r2 = x1 * sin + x2 * cos
            return jnp.stack([r1, r2], axis=-1).reshape(x.shape)

        def _decay_matrix(S):
            gammas = 1.0 - jnp.exp(jnp.linspace(np.log(1 / 32), np.log(1 / 64), H)).astype(jnp.float32)
            n = jnp.arange(S)
            diff = (n[:, None] - n[None, :]).astype(jnp.float32)
            pw = jnp.exp(jnp.clip(diff, 0.0)[None] * jnp.log(gammas)[:, None, None])
            return jnp.where(diff[None] >= 0, pw, 0.0)

        def _retention(x, Wq, Wk, Wv, Wg, Wo, gn_s, gn_b, Dm, cos, sin):
            B, S, _ = x.shape
            Q = (x @ Wq).reshape(B, S, H, DH)
            K = (x @ Wk).reshape(B, S, H, DH)
            V = (x @ Wv).reshape(B, S, H, DH)
            Q = _rotate(Q, cos, sin)
            K = _rotate(K, cos, -sin)
            att = jnp.einsum('bnhd,bmhd->bhnm', Q, K) * Dm
            Y = jnp.einsum('bhnm,bmhd->bnhd', att, V)
            mu = Y.mean(-1, keepdims=True)
            var = Y.var(-1, keepdims=True)
            Y = (Y - mu) * jax.lax.rsqrt(var + EPS)
            Y = Y.reshape(B, S, D) * gn_s + gn_b
            G = jax.nn.swish(x @ Wg)
            return G * Y @ Wo
        key = jax.random.key(seed)
        ks = jax.random.split(key, 8)
        B, S = (4, 128)
        sd = 1.0 / np.sqrt(D)
        sf = 1.0 / np.sqrt(F)
        return {'X': jax.random.normal(ks[0], (B, S, D), jnp.float32), 'Wq': jax.random.normal(ks[1], (L, D, D), jnp.float32) * sd, 'Wk': jax.random.normal(ks[2], (L, D, D), jnp.float32) * sd, 'Wv': jax.random.normal(ks[3], (L, D, D), jnp.float32) * sd, 'Wg': jax.random.normal(ks[4], (L, D, D), jnp.float32) * sd, 'Wo': jax.random.normal(ks[5], (L, D, D), jnp.float32) * sd, 'W1': jax.random.normal(ks[6], (L, D, F), jnp.float32) * sd, 'W2': jax.random.normal(ks[7], (L, F, D), jnp.float32) * sf, 'ln_scale': jnp.ones((D,), jnp.float32), 'ln_bias': jnp.zeros((D,), jnp.float32), 'gn_scale': jnp.ones((L, D), jnp.float32), 'gn_bias': jnp.zeros((L, D), jnp.float32)}
    _L0_attn_in = _L0_attn_setup()

    def _L0_ffn_setup():
        import jax, jax.numpy as jnp
        import numpy as np
        CAPACITY_FACTOR = 1.25
        key = jax.random.key(seed)
        k1, k2, k3, k4 = jax.random.split(key, 4)
        B, T, D, F, E = (4, 512, 128, 512, 8)
        s = 0.02
        return {'x': jax.random.normal(k1, (B, T, D), dtype=jnp.float32), 'wg': jax.random.normal(k2, (D, E), dtype=jnp.float32) * s, 'W1': jax.random.normal(k3, (E, D, F), dtype=jnp.float32) * s, 'b1': jnp.zeros((E, F), dtype=jnp.float32), 'W2': jax.random.normal(k4, (E, F, D), dtype=jnp.float32) * s, 'b2': jnp.zeros((E, D), dtype=jnp.float32)}
    _L0_ffn_in = _L0_ffn_setup()
    _d = {'L0_attn_X': _L0_attn_in['X'], 'L0_attn_Wq': _L0_attn_in['Wq'], 'L0_attn_Wk': _L0_attn_in['Wk'], 'L0_attn_Wv': _L0_attn_in['Wv'], 'L0_attn_Wg': _L0_attn_in['Wg'], 'L0_attn_Wo': _L0_attn_in['Wo'], 'L0_attn_W1': _L0_attn_in['W1'], 'L0_attn_W2': _L0_attn_in['W2'], 'L0_attn_ln_scale': _L0_attn_in['ln_scale'], 'L0_attn_ln_bias': _L0_attn_in['ln_bias'], 'L0_attn_gn_scale': _L0_attn_in['gn_scale'], 'L0_attn_gn_bias': _L0_attn_in['gn_bias'], 'L0_ffn_wg': _L0_ffn_in['wg'], 'L0_ffn_W1': _L0_ffn_in['W1'], 'L0_ffn_b1': _L0_ffn_in['b1'], 'L0_ffn_W2': _L0_ffn_in['W2'], 'L0_ffn_b2': _L0_ffn_in['b2']}
    _x0 = _d['L0_attn_X']
    _d['L0_attn_X'] = jax.random.normal(jax.random.fold_in(jax.random.key(seed), 1), (2, 2048, 128), dtype=_x0.dtype)
    del _x0
    return _d

def reference(L0_attn_X, L0_attn_Wq, L0_attn_Wk, L0_attn_Wv, L0_attn_Wg, L0_attn_Wo, L0_attn_W1, L0_attn_W2, L0_attn_ln_scale, L0_attn_ln_bias, L0_attn_gn_scale, L0_attn_gn_bias, L0_ffn_wg, L0_ffn_W1, L0_ffn_b1, L0_ffn_W2, L0_ffn_b2):

    def _L0_attn_ref(X, Wq, Wk, Wv, Wg, Wo, W1, W2, ln_scale, ln_bias, gn_scale, gn_bias):
        import jax, jax.numpy as jnp
        import numpy as np
        L, D, F, H = (4, 128, 256, 8)
        DH = D // H
        EPS = 1e-05

        def _layer_norm(x, scale, bias):
            mu = x.mean(-1, keepdims=True)
            var = x.var(-1, keepdims=True)
            return (x - mu) * jax.lax.rsqrt(var + EPS) * scale + bias

        def _rotate(x, cos, sin):
            x1, x2 = (x[..., 0::2], x[..., 1::2])
            r1 = x1 * cos - x2 * sin
            r2 = x1 * sin + x2 * cos
            return jnp.stack([r1, r2], axis=-1).reshape(x.shape)

        def _decay_matrix(S):
            gammas = 1.0 - jnp.exp(jnp.linspace(np.log(1 / 32), np.log(1 / 64), H)).astype(jnp.float32)
            n = jnp.arange(S)
            diff = (n[:, None] - n[None, :]).astype(jnp.float32)
            pw = jnp.exp(jnp.clip(diff, 0.0)[None] * jnp.log(gammas)[:, None, None])
            return jnp.where(diff[None] >= 0, pw, 0.0)

        def _retention(x, Wq, Wk, Wv, Wg, Wo, gn_s, gn_b, Dm, cos, sin):
            B, S, _ = x.shape
            Q = (x @ Wq).reshape(B, S, H, DH)
            K = (x @ Wk).reshape(B, S, H, DH)
            V = (x @ Wv).reshape(B, S, H, DH)
            Q = _rotate(Q, cos, sin)
            K = _rotate(K, cos, -sin)
            att = jnp.einsum('bnhd,bmhd->bhnm', Q, K) * Dm
            Y = jnp.einsum('bhnm,bmhd->bnhd', att, V)
            mu = Y.mean(-1, keepdims=True)
            var = Y.var(-1, keepdims=True)
            Y = (Y - mu) * jax.lax.rsqrt(var + EPS)
            Y = Y.reshape(B, S, D) * gn_s + gn_b
            G = jax.nn.swish(x @ Wg)
            return G * Y @ Wo
        B, S, _ = X.shape
        pos = jnp.arange(S, dtype=jnp.float32)
        inv_freq = 1.0 / 10000.0 ** (jnp.arange(0, DH, 2, dtype=jnp.float32) / DH)
        ang = pos[:, None] * inv_freq[None, :]
        cos = jnp.cos(ang)[None, :, None, :]
        sin = jnp.sin(ang)[None, :, None, :]
        Dm = _decay_matrix(S)
        for i in range(L):
            Yr = _retention(_layer_norm(X, ln_scale, ln_bias), Wq[i], Wk[i], Wv[i], Wg[i], Wo[i], gn_scale[i], gn_bias[i], Dm, cos, sin) + X
            X = jax.nn.gelu(_layer_norm(Yr, ln_scale, ln_bias) @ W1[i]) @ W2[i] + Yr
        return X

    def _L0_ffn_ref(x, wg, W1, b1, W2, b2):
        import jax, jax.numpy as jnp
        import numpy as np
        CAPACITY_FACTOR = 1.25
        B, T, D = x.shape
        E = wg.shape[1]
        N = B * T
        capacity = int(N / E * CAPACITY_FACTOR) + 1
        xf = x.reshape(N, D)
        logits = xf @ wg
        scores = jax.nn.softmax(logits, axis=-1)
        top1 = jnp.argmax(scores, axis=-1)
        combine_w = jnp.take_along_axis(scores, top1[:, None], axis=1)[:, 0]
        oh = jax.nn.one_hot(top1, E, dtype=jnp.int32)
        rank = jnp.take_along_axis(jnp.cumsum(oh, axis=0), top1[:, None], axis=1)[:, 0] - 1
        valid = rank < capacity
        trash = E * capacity
        slot = jnp.where(valid, top1 * capacity + rank, trash)
        buf = jnp.zeros((E * capacity + 1, D), dtype=x.dtype).at[slot].set(xf)
        eb = buf[:E * capacity].reshape(E, capacity, D)
        h = jax.nn.gelu(jnp.einsum('ecd,edf->ecf', eb, W1) + b1[:, None, :], approximate=False)
        y = jnp.einsum('ecf,efd->ecd', h, W2) + b2[:, None, :]
        yf = y.reshape(E * capacity, D)
        gathered = yf[jnp.minimum(slot, E * capacity - 1)]
        out_flat = jnp.where(valid[:, None], gathered, 0.0) * combine_w[:, None]
        return out_flat.reshape(B, T, D)
    x = L0_attn_X
    xn = _layernorm(x, axis=-1)
    x = x + _L0_attn_ref(xn, L0_attn_Wq, L0_attn_Wk, L0_attn_Wv, L0_attn_Wg, L0_attn_Wo, L0_attn_W1, L0_attn_W2, L0_attn_ln_scale, L0_attn_ln_bias, L0_attn_gn_scale, L0_attn_gn_bias) + _L0_ffn_ref(xn, L0_ffn_wg, L0_ffn_W1, L0_ffn_b1, L0_ffn_W2, L0_ffn_b2)
    return x

_drawn_inputs = setup_inputs


def setup_inputs(seed=0):
    import zlib

    import numpy as np

    out = dict(_drawn_inputs(seed))
    spreads = {'L0_attn_ln_scale': (1.0, 0.2),
     'L0_attn_ln_bias': (0.0, 0.1),
     'L0_attn_gn_scale': (1.0, 0.2),
     'L0_attn_gn_bias': (0.0, 0.1),
     'L0_ffn_b1': (0.0, 0.8),
     'L0_ffn_b2': (0.0, 0.8)}
    factors = {'L0_ffn_wg': 8.0, 'L0_ffn_W1': 8.0, 'L0_ffn_W2': 8.0}
    for name, (base, spread) in spreads.items():
        noise = np.random.default_rng([zlib.crc32(name.encode()), seed]).standard_normal(out[name].shape)
        drawn = base * np.exp(spread * noise) if base else spread * noise
        out[name] = jnp.asarray(drawn.astype(out[name].dtype))
    for name, factor in factors.items():
        out[name] = (out[name] * factor).astype(out[name].dtype)
    return out
```

```python
from contextlib import ExitStack

import numpy as np

import concourse.bass as bass
from concourse import mybir
from concourse.alu_op_type import AluOpType as ALU

F32 = mybir.dt.float32
I32 = mybir.dt.int32
U32 = mybir.dt.uint32
ACT = mybir.ActivationFunctionType
AX = mybir.AxisListType

P = 128
GC = 4
GT = GC * P
EPS = 1e-5

IDENT = 0
TRI = IDENT + P
ONES = TRI + P
BLOCKDEC = ONES + P
HEADMASK = BLOCKDEC + P
BLOCKMEAN = HEADMASK + 4
DECAY = BLOCKMEAN + 8
KEEP = DECAY + 1
DECKEEP = KEEP + 4
REVEXP = DECKEEP + 4
NOTFIRST = REVEXP + 8
CONSTS = NOTFIRST + 8 * 32


def shape_constants(S, H, DH):
    D = H * DH
    half = DH // 2
    f32 = np.float32
    ends = np.log(1 / 32), np.log(1 / 64)
    gam = (1.0 - np.exp(np.linspace(ends[0], ends[1], H).astype(f32))).astype(f32)
    lg = np.log(gam).astype(f32).astype(np.float64)
    inv = (f32(1.0) / np.power(f32(10000.0), np.arange(0, DH, 2, dtype=f32) / f32(DH))).astype(f32)
    ang = (np.arange(S, dtype=f32)[:, None] * inv[None, :]).astype(f32).astype(np.float64)
    cos, sin = np.cos(ang), np.sin(ang)
    within = np.arange(S) % P
    qd = np.exp(within[:, None] * lg)
    kd = np.exp(-within[:, None] * lg)

    def table(first, second, decay):
        t = np.concatenate([first, second], axis=1)[:, None, :] * decay[:, :, None]
        return t.reshape(S, D)

    rope_c = np.concatenate([table(cos, cos, qd), table(cos, cos, kd)], axis=1)
    rope_s = np.concatenate([table(-sin, sin, qd), table(sin, -sin, kd)], axis=1)
    rope_c, rope_s = (
        np.ascontiguousarray(t.reshape(S // P, P, 2 * D).transpose(1, 0, 2)).astype(f32)
        for t in (rope_c, rope_s)
    )
    c = np.zeros((P, CONSTS), f32)
    feat = np.arange(P) // DH
    dec = np.exp(P * lg)[feat]
    c[:, IDENT:IDENT + P] = np.eye(P)
    c[:, TRI:TRI + P] = np.triu(np.ones((P, P)))
    c[:, ONES:ONES + P] = 1.0
    c[:, BLOCKDEC:BLOCKDEC + P] = (feat[:, None] == feat[None, :]) * dec[:, None]
    for v in range(4):
        c[:, HEADMASK + v] = feat % 4 == v
    for h in range(H):
        c[:, BLOCKMEAN + h] = (feat == h) / DH
    c[:, DECAY] = dec
    for g in range(4):
        c[:, KEEP + g] = g > 0
        c[:, DECKEEP + g] = dec * (g > 0)
    c[:, REVEXP:REVEXP + 8] = 8 - np.arange(8)
    c[:, NOTFIRST:] = np.tile(np.arange(32) > 0, 8)
    return c, rope_c, rope_s


def retention_moe(nc, x, wqkv, wg, wo, w1, w2, ln, gn, gate, ew1, eb1, ew2, eb2,
                  consts, rope_c, rope_s, out):
    NTOK, D = x.shape
    NCH = NTOK // P
    NG = NCH // GC
    SCH = rope_c.shape[1]
    L = wo.shape[1]
    H, DH = 8, 16
    E, _, FE = ew1.shape
    FB = FE // P
    CAP = int(NTOK / E * 1.25) + 1
    FULL = CAP // P
    TAIL = CAP - FULL * P
    assert D == P and TAIL == 1 and FULL == 5 and NG == 8 and L == 4
    STEPS = L * NG
    PARAMS = 16 * 11

    with ExitStack() as ctx:
        def sb(name, shape, dt=F32):
            return ctx.enter_context(nc.sbuf_tensor(name, shape, dt))

        def sem(name):
            return ctx.enter_context(nc.semaphore(name))

        def sems(name, n):
            return [sem(f"{name}{i}") for i in range(n)]

        bank = [ctx.enter_context(nc.psum_tensor(f"bank{i}", [P, 512], F32)) for i in range(8)]

        cst = sb("cst", [P, CONSTS])
        ident, tri, ones = (cst[:, o:o + P] for o in (IDENT, TRI, ONES))
        blockdec = cst[:, BLOCKDEC:BLOCKDEC + P]
        blockmean = cst[:, BLOCKMEAN:BLOCKMEAN + H]
        xin = sb("xin", [P, NCH, D])
        res = sb("res", [P, NCH, D])
        ropec = sb("ropec", [P, SCH, 2 * D])
        ropes = sb("ropes", [P, SCH, 2 * D])
        wqkv_all = sb("wqkv_all", [P, L, 3 * D])
        wg_all = sb("wg_all", [P, L, D])
        wo_all = sb("wo_all", [P, L, D])
        w1_all = sb("w1_all", [P, L, 2 * D])
        w2_all = sb("w2_all", [P, L, 2 * D])
        ln_sb = sb("ln_sb", [P, 2])
        gn_sb = sb("gn_sb", [P, 2 * L])
        power = sb("power", [P, 32])
        stats = sb("stats", [P, 8, 6])
        routed = sb("routed", [P, NCH, D])
        weight = sb("weight", [P, NCH])
        slots = sb("slots", [P, NCH], U32)

        xhat = sb("xhat", [P, GC, D])
        xT = sb("xT", [P, GT])
        xhat2 = sb("xhat2", [P, GC, D])
        x2T = sb("x2T", [P, GT])
        wg_now = sb("wg_now", [P, D])
        w1_now = sb("w1_now", [P, 2 * D])
        gateT = sb("gateT", [P, 4, GT])
        rc = sb("rc", [P, 2, 2 * D])
        rs_ = sb("rs_", [P, 2, 2 * D])
        qk = sb("qk", [P, 2, GC, 2 * D])
        vpad = sb("vpad", [P, 2, GC, 2 * D])
        qT = sb("qT", [P, 2, 5, GT])
        kT = sb("kT", [P, 2, GT])
        probs = sb("probs", [P, 2, 2, GT])
        state = sb("state", [P, D])
        smask = sb("smask", [P, 2, D])
        ysb = sb("ysb", [P, GT])
        ysq = sb("ysq", [P, GT])
        var8 = sb("var8", [H, GT])
        vare = sb("vare", [P, GC * H])
        rstd = sb("rstd", [P, GC * H])
        rstdx = sb("rstdx", [P, GT])
        z1 = sb("z1", [P, GT])
        zT = sb("zT", [P, GT])
        hT = sb("hT", [P, 2, GT])
        mv1 = sb("mv1", [P, GC, 2])
        ve1 = sb("ve1", [P, GC])
        rs1 = sb("rs1", [P, GC])
        mv2 = sb("mv2", [P, GC, 2])
        ve2 = sb("ve2", [P, GC])
        rs2 = sb("rs2", [P, GC])

        gw_sb = sb("gw_sb", [P, E])
        b1_sb = sb("b1_sb", [P, E * FB])
        mv0 = sb("mv0", [P, NCH, 2])
        ve0 = sb("ve0", [P, NCH])
        rs0 = sb("rs0", [P, NCH])
        xnT = [qT[:, 0, k, :] for k in range(2)]
        lT = [qT[0:E, 0, 2 + k, :] for k in range(2)]
        gt = {n: qT[:, 1, i // 2, 256 * (i % 2):256 * (i % 2) + 256] for i, n in enumerate(
            ("logit", "shifted", "exp", "equal", "score", "onehot", "scan", "rank"))}
        g_prod = kT[:, 0, 0:256]
        zeros = sb("zeros", [P, CAP])
        gsm = {n: sb("g_" + n, [P, NCH]) for n in ("max", "sum", "inv", "rev", "rank", "kept", "slot", "far")}
        e_w1 = [gateT[:, k, :] for k in range(2)]
        e_w2 = [gateT[:, 2 + k, :].rearrange("p (f d) -> p f d", d=D) for k in range(2)]
        e_b2 = [z1[:, D * k:D * k + D] for k in range(2)]
        e_x = [qk[:, 0, :, :], qk[:, 1, :, :]]
        e_x = [t.rearrange("p a (b d) -> p (a b) d", d=D)[:, 0:FULL + 1, :] for t in e_x]
        e_y = [vpad[:, k, :, :].rearrange("p a (b d) -> p (a b) d", d=D)[:, 0:FULL + 1, :] for k in range(2)]
        e_xT = [qT[:, 0, 2 * k:2 * k + 2, :].rearrange("p a n -> p (a n)")[:, 0:CAP] for k in range(2)]
        e_hT = sb("e_hT", [P, FB, CAP])

        slot_x = nc.dram_tensor("slot_x", [E * CAP, D], F32, kind="Internal").ap()
        slot_y = nc.dram_tensor("slot_y", [E * CAP, D], F32, kind="Internal").ap()
        x_dram = x.rearrange("(c p) d -> p c d", p=P)
        out_dram = out.rearrange("(c p) d -> p c d", p=P)

        d_const, d_params, d_rope, d_zero, d_scatter, d_gather = (
            sem(n) for n in ("d_const", "d_params", "d_rope", "d_zero", "d_scatter", "d_gather"))
        d_x = sems("d_x", 4)
        d_ew, d_ex, d_ey = sems("d_ew", 2), sems("d_ex", 2), sems("d_ey", 2)
        d_out = sem("d_out")
        zeroed, cleared, v_centred, prepared, ln0_var, ln0_rstd, ln0_done = (
            sem(n) for n in ("zeroed", "cleared", "v_centred", "prepared", "ln0_var", "ln0_rstd", "ln0_done"))
        g_xT_psum, g_xT_ready, g_lT_psum, g_lT_ready, g_logits, g_shifted, g_exp, g_onehot, g_ranks, g_slots, \
            chained = (sem(n) for n in ("g_xT_psum", "g_xT_ready", "g_lT_psum", "g_lT_ready", "g_logits",
                                        "g_shifted", "g_exp", "g_onehot", "g_ranks", "g_slots", "chained"))
        e_rows_psum, e_xT_ready, e_y_psum, e_y_ready = (
            sems(n, 2) for n in ("e_rows_psum", "e_xT_ready", "e_y_psum", "e_y_ready"))
        e_ha_psum, e_hb_psum, e_ha_ready, e_hb_ready = (
            sems(n, FB) for n in ("e_ha_psum", "e_hb_psum", "e_ha_ready", "e_hb_ready"))
        t1_psum, t2_psum, var_psum, g_psum, vt_psum, w1a_psum, w1b_psum, rt_psum, w2_psum, wo_psum, \
            tq_psum, tk_psum, y_psum = (sem(n + "_psum") for n in (
                "t1", "t2", "var", "g", "vt", "w1a", "w1b", "rt", "w2", "wo", "tq", "tk", "y"))
        xhat_ready, xT_ready, x2hat_ready, x2T_ready, var8_ready, gate_ready, vare_ready, rstd_ready, \
            ha_ready, hb_ready, z1_ready, zT_ready, ffn_added, attn_added, qT_ready, kT_ready, y_ready, \
            wg_ready, w1_ready, ln1_var, ln1_rstd, ln2_var, ln2_rstd, ln1_st, ln2_st, ln1_mv, ln2_mv, rstdx_ready = (sem(n) for n in (
                "xhat_ready", "xT_ready", "x2hat_ready", "x2T_ready", "var8_ready", "gate_ready", "vare_ready",
                "rstd_ready", "ha_ready", "hb_ready", "z1_ready", "zT_ready", "ffn_added", "attn_added",
                "qT_ready", "kT_ready", "y_ready", "wg_ready", "w1_ready", "ln1_var", "ln1_rstd", "ln2_var",
                "ln2_rstd", "ln1_st", "ln2_st", "ln1_mv", "ln2_mv", "rstdx_ready"))
        att_psum, probs_ready, av_done, kvq_psum, v_ready, smask_ready, state_ready, kvq_read, qk_ready = (
            sems(n, GC) for n in ("att_psum", "probs_ready", "av_done", "kvq_psum", "v_ready", "smask_ready",
                                  "state_ready", "kvq_read", "qk_ready"))
        passed = {e: sem(f"passed_{e.value}") for e in (nc.tensor.engine, nc.scalar.engine, nc.vector.engine)}
        summed, out_ready = sem("summed"), sem("out_ready")

        USES = [
            ("t1", 1, xT_ready), ("var", -1, var8_ready), ("g", 1, gate_ready), ("t2", -2, x2T_ready),
            ("vt", -1, vare_ready), ("w1a", -2, ha_ready), ("w1b", -2, hb_ready), ("rt", -1, z1_ready),
            ("w2", -2, ffn_added), ("wo", -1, attn_added), ("tq", 1, qT_ready), ("tk", 1, kT_ready),
        ]
        PLACE = {name: i for i, (name, _, _) in enumerate(USES)}

        def ring_bank(name):
            return bank[5 + PLACE[name] % 3]

        def before(name, t):
            k = PLACE[name] - 3
            while True:
                who, off, s = USES[k % len(USES)]
                off += k // len(USES)
                if not isinstance(t, int):
                    return s, off
                if k // len(USES) + t < -1:
                    return None
                if 0 <= t + off < STEPS:
                    return s, off
                k -= 3

        class Counts:

            def __init__(self, eng, t):
                self.t, self.fixed = t, isinstance(t, int)
                self.reg = None if self.fixed else {k: eng.snap(t + (k + 1)) for k in range(-3, 3)}

            def __call__(self, k):
                return self.t + k + 1 if self.fixed else self.reg[k]

        def need(eng, s, value):
            if not isinstance(value, int) or value > 0:
                eng.wait_ge(s, value)

        def need_alone(eng, s, value):
            need(eng, s, value)
            if not isinstance(value, int):
                eng.sem_inc(passed[eng.engine], 1)

        def stages(t):
            if not isinstance(t, int):
                return True, True, True, True
            return tuple(0 <= t + k < STEPS for k in (1, 0, -1, -2))

        FIRST, LAST = 4, STEPS - 3
        assert (LAST - FIRST + 1) % 2 == 0

        def run_steps(eng, step):
            for t in range(-1, FIRST):
                step(t, t % 2, Counts(eng, t))
            with eng.Fori(0, (LAST - FIRST + 1) // 2) as i:
                for k in range(2):
                    t = i * 2 + (FIRST + k)
                    step(t, (FIRST + k) % 2, Counts(eng, t))
            for t in range(LAST + 1, STEPS + 2):
                step(t, t % 2, Counts(eng, t))

        def run_experts(eng, expert):
            expert(0, 0, Counts(eng, 0))
            with eng.Fori(0, (E - 2) // 2) as i:
                for k in range(2):
                    e = i * 2 + (1 + k)
                    expert(e, (1 + k) % 2, Counts(eng, e))
            expert(E - 1, (E - 1) % 2, Counts(eng, E - 1))

        def layer_of(i):
            return (i // NG) if isinstance(i, int) else (i >> 3) & (L - 1)

        def group_of(i):
            return i % NG if isinstance(i, int) else i & (NG - 1)

        def row(ap, i):
            return ap[:, i:i + 1] if isinstance(i, int) else ap[:, bass.ds(i, 1)]

        def group_rows(ap, i):
            g = group_of(i)
            if isinstance(g, int):
                return ap[:, GC * g:GC * g + GC, :]
            return ap[:, bass.ds(g * GC, GC), :]

        def chunk_row(ap, i, j):
            c = (group_of(i) & (ap.shape[1] // GC - 1)) * GC + j
            return row(ap, c)

        def cols(j, n=P):
            return slice(n * j, n * j + n)

        def flat(ap):
            return ap.rearrange("p a b -> p (a b)")

        def padded_heads(ap):
            return ap.rearrange("p (r w d) -> p r w d", r=4, d=DH)[:, :, 0:4:3, :]

        block = ctx.enter_context(nc.Block())

        @block.sync
        def _(sp):
            sp.dma_start(cst[:], consts).then_inc(d_const, 16)
            for k in range(4):
                sp.dma_start(xin[:, cols(k, 8), :], x_dram[:, cols(k, 8), :]).then_inc(d_x[k], 16)
            sp.wait_ge(zeroed, 1)
            slot_rows = slot_x.rearrange("r d -> (r d)").rearrange("(p k) -> p k", p=P)
            for k in range(E * CAP * D // P // CAP):
                sp.dma_start(slot_rows[:, cols(k, CAP)], zeros[:, :]).then_inc(d_zero, 16)

            def load_weights(e, par):
                a = ew1[bass.ds(e, 1)] if not isinstance(e, int) else ew1[e:e + 1]
                b = ew2[bass.ds(e, 1)] if not isinstance(e, int) else ew2[e:e + 1]
                d = eb2[bass.ds(e, 1)] if not isinstance(e, int) else eb2[e:e + 1]
                sp.dma_start(e_w1[par], a.rearrange("a p f -> (a p) f")).then_inc(d_ew[par], 16)
                sp.dma_start(e_w2[par], b.rearrange("a (f p) d -> p (a f) d", p=P)).then_inc(d_ew[par], 16)
                sp.dma_start(e_b2[par], d.rearrange("a d -> (a d)").partition_broadcast(P)).then_inc(d_ew[par], 16)

            slot_tiles = slot_x.rearrange("(e r) d -> e r d", e=E)

            def load_rows(e, par):
                src = slot_tiles[e:e + 1] if isinstance(e, int) else slot_tiles[bass.ds(e, 1)]
                sp.dma_start(e_x[par][:, 0:FULL, :], src[:, 0:FULL * P, :].rearrange(
                    "a (i p) d -> p (a i) d", p=P)).then_inc(d_ex[par], 16)
                sp.dma_start(e_x[par][0:1, FULL, :], src[:, FULL * P:CAP, :].rearrange(
                    "a r d -> (a r) d")).then_inc(d_ex[par], 16)

            load_weights(0, 0)
            load_weights(1, 1)
            sp.wait_ge(d_scatter, 16 * NCH)
            load_rows(0, 0)
            load_rows(1, 1)
            with sp.Fori(0, (E - 2) // 2) as i:
                for k in range(2):
                    e = i * 2 + k
                    sp.wait_ge(e_y_ready[1], e + 1)
                    load_weights(e + 2, k)
                    load_rows(e + 2, k)

            for g in range(NG):
                sp.wait_ge(out_ready, g + 1)
                sp.dma_start(out_dram[:, cols(g, GC), :], xin[:, cols(g, GC), :]).then_inc(d_out, 16)
            sp.wait_ge(d_out, 16 * NG)

        @block.tensor
        def _(pe):
            def transpose(dst, src, last=None):
                mm = pe.transpose(dst, src, ident[0:src.shape[0], 0:src.shape[0]])
                if last is not None:
                    mm.then_inc(last, 1)

            def mm(dst, lhsT, rhs, start=True, stop=True):
                return pe.matmul(dst, lhsT, rhs, start=start, stop=stop)

            pe.wait_ge(d_const, 16)
            for g in range(NG):
                if g % 2 == 0:
                    pe.wait_ge(ln0_done, g // 2 + 1)
                if g >= 2:
                    pe.wait_ge(g_xT_ready, g - 1)
                for j in range(GC):
                    transpose(bank[g % 2][:, cols(j)], res[:, GC * g + j, :], g_xT_psum if j == GC - 1 else None)
                if g == 0:
                    pe.wait_ge(d_params, PARAMS)
                pe.wait_ge(g_xT_ready, g + 1)
                if g >= 2:
                    pe.wait_ge(g_lT_ready, g - 1)
                mm(bank[2 + g % 2][0:E, :], gw_sb[:, :], xnT[g % 2]).then_inc(g_lT_psum, 1)
                pe.wait_ge(g_lT_ready, g + 1)
                for j in range(GC):
                    c = GC * g + j
                    transpose(bank[4][:, cols(c, E)], lT[g % 2][:, cols(j)], g_logits if c == NCH - 1 else None)
            pe.wait_ge(g_onehot, 1)
            mm(bank[5][:, 0:256], tri, gt["onehot"])
            mm(bank[6][:, 0:256], ones, gt["onehot"]).then_inc(g_ranks, 1)

            def expert(e, par, n):
                def rows(x, parity, k):
                    pe.wait_ge(d_ex[parity], k)
                    for i in range(GC):
                        transpose(bank[0][:, cols(i)], x[:, i, :], e_rows_psum[0] if i == GC - 1 else None)
                    transpose(bank[1][:, 0:P], x[:, GC, :])
                    mm(bank[1][:, P:P + 1], x[0:1, FULL, :], ones[0:1, 0:1]).then_inc(e_rows_psum[1], 1)

                first = isinstance(e, int) and e == 0
                final = isinstance(e, int) and e == E - 1
                half = (e >> 1) if not isinstance(e, int) else e // 2
                if first:
                    rows(e_x[0], 0, 32)
                pe.wait_ge(d_ew[par], (half + 1) * 48)
                for f in range(FB):
                    w = e_w1[par][:, cols(f)]
                    if f == 0:
                        pe.wait_ge(e_xT_ready[0], n(0))
                    need(pe, e_ha_ready[(f + 2) % FB], n(0) if f >= 2 else n(-1))
                    mm(bank[2 + f % 2][:, :], w, e_xT[par][:, 0:GT]).then_inc(e_ha_psum[f], 1)
                    if f == 0:
                        pe.wait_ge(e_xT_ready[1], n(0))
                    need(pe, e_hb_ready[(f + 2) % FB], n(0) if f >= 2 else n(-1))
                    mm(bank[4 + f % 2][:, 0:CAP - GT], w, e_xT[par][:, GT:CAP]).then_inc(e_hb_psum[f], 1)
                if not final:
                    rows(e_x[1 - par], 1 - par, (((e + 1) >> 1) + 1) * 32)
                need(pe, e_y_ready[0], n(-1))
                for i in range(FULL + 1):
                    m = P if i < FULL else TAIL
                    dst = bank[6][:, cols(i)] if i < GC else bank[7][0:m, cols(i - GC)]
                    if i == GC:
                        need(pe, e_y_ready[1], n(-1))
                    for f in range(FB):
                        if i == 0:
                            pe.wait_ge(e_ha_ready[f], n(0))
                        if i == GC:
                            pe.wait_ge(e_hb_ready[f], n(0))
                        last = mm(dst, e_hT[:, f, P * i:P * i + m], e_w2[par][:, f, :], f == 0, f == FB - 1)
                    if i == GC - 1:
                        last.then_inc(e_y_psum[0], 1)
                last.then_inc(e_y_psum[1], 1)

            run_experts(pe, expert)

            def free(name, t, n):
                got = before(name, t)
                if got is not None:
                    need(pe, got[0], n(got[1]))

            def kvq(t, par, n, j, s1, s2):
                b = bank[2 + j % 2]
                need(pe, kvq_read[(j + 2) % GC], n(1) if j >= 2 else n(0))
                if s2:
                    pe.wait_ge(v_ready[j], n(0))
                    last = mm(b[:, 3 * P:4 * P], qk[:, par, j, P:2 * P], padded_heads(vpad[:, par, j, :]))
                if s1:
                    last = mm(b[:, 0:3 * P], xT[:, cols(j)], row(wqkv_all, layer_of(t + 1)))
                last.then_inc(kvq_psum[j], 1)

            def att(par, n, j):
                need_alone(pe, probs_ready[(j + 3) % GC], n(0) if j else n(-1))
                if j == 0:
                    pe.wait_ge(qT_ready, n(0))
                    need_alone(pe, kT_ready, n(0))
                h = P // 2
                for q in range(2):
                    r = slice(h * q, h * q + h)
                    dst = bank[q][:, :].rearrange("p (v n) -> p v n", v=4)
                    mm(bank[q][0:h, :], kT[r, par, P * j:P * j + h], qT[r, par, 0:4, cols(j)])
                    last = mm(dst[h:P, :, h:P], kT[r, par, P * j + h:P * j + P], qT[r, par, 0:4, P * j + h:P * j + P])
                last.then_inc(att_psum[j], 1)

            def av(par, n, j):
                if j == 0:
                    need(pe, y_ready, n(-1))
                dst = bank[4][:, cols(j)]
                pe.wait_ge(smask_ready[j], n(0))
                pe.matmul(dst, smask[:, j % 2, :], qT[:, par, 4, cols(j)], start=True, stop=False,
                          skip_group_check=True)
                pe.wait_ge(probs_ready[j], n(0))
                for h in range(H):
                    r = h // 2
                    last = pe.matmul(dst[32 * r:32 * r + 32, :], vpad[:, par, j, cols(h, 32)],
                                     probs[:, j % 2, h // 4, cols(h % 4)], start=False, stop=h % 2 == 1,
                                     tile_position=(0, 32 * r), skip_group_check=True)
                last.then_inc(av_done[j], 1)

            def step(t, par, n):
                s1, s2, s3, s4 = stages(t)
                if s1:
                    free("t1", t, n)
                    pe.wait_ge(xhat_ready, n(1))
                    for j in range(GC):
                        transpose(ring_bank("t1")[:, cols(j)], xhat[:, j, :], t1_psum if j == GC - 1 else None)
                if s3:
                    free("var", t, n)
                    pe.wait_ge(y_ready, n(-1))
                    mm(ring_bank("var")[0:H, :], blockmean, ysq[:, :]).then_inc(var_psum, 1)
                if s2:
                    att(par, n, 0)
                if s1:
                    free("g", t, n)
                    pe.wait_ge(xT_ready, n(1))
                    pe.wait_ge(wg_ready, n(1))
                    mm(ring_bank("g")[:, :], wg_now[:, :], xT[:, :]).then_inc(g_psum, 1)
                if s1 or s2:
                    kvq(t, par, n, 0, s1, s2)
                if s4:
                    free("t2", t, n)
                    pe.wait_ge(x2hat_ready, n(-2))
                    for j in range(GC):
                        transpose(ring_bank("t2")[:, cols(j)], xhat2[:, j, :], t2_psum if j == GC - 1 else None)
                if s3:
                    free("vt", t, n)
                    need_alone(pe, var8_ready, n(-1))
                    for j in range(GC):
                        transpose(ring_bank("vt")[:, cols(j, H)], var8[:, cols(j)], vt_psum if j == GC - 1 else None)
                if s2:
                    att(par, n, 1)
                    av(par, n, 0)
                if s1 or s2:
                    kvq(t, par, n, 1, s1, s2)
                if s4:
                    free("w1a", t, n)
                    pe.wait_ge(x2T_ready, n(-2))
                    pe.wait_ge(w1_ready, n(-2))
                    mm(ring_bank("w1a")[:, :], w1_now[:, 0:P], x2T[:, :]).then_inc(w1a_psum, 1)
                if s2:
                    att(par, n, 2)
                    av(par, n, 1)
                if s1 or s2:
                    kvq(t, par, n, 2, s1, s2)
                if s4:
                    free("w1b", t, n)
                    mm(ring_bank("w1b")[:, :], w1_now[:, P:2 * P], x2T[:, :]).then_inc(w1b_psum, 1)
                if s3:
                    free("rt", t, n)
                    pe.wait_ge(rstdx_ready, n(-1))
                    for j in range(GC):
                        transpose(ring_bank("rt")[:, cols(j)], rstdx[:, cols(j)], rt_psum if j == GC - 1 else None)
                if s2:
                    att(par, n, 3)
                    av(par, n, 2)
                if s1 or s2:
                    kvq(t, par, n, 3, s1, s2)
                if s4:
                    free("w2", t, n)
                    pe.wait_ge(ha_ready, n(-2))
                    pe.wait_ge(hb_ready, n(-2))
                    wl = row(w2_all, layer_of(t - 2))
                    for j in range(GC):
                        for f in range(2):
                            last = mm(ring_bank("w2")[:, cols(j)], hT[:, f, cols(j)], wl[:, :, cols(f)], f == 0, f == 1)
                    last.then_inc(w2_psum, 1)
                if s3:
                    free("wo", t, n)
                    pe.wait_ge(zT_ready, n(-1))
                    for j in range(GC):
                        last = mm(ring_bank("wo")[:, cols(j)], zT[:, cols(j)], row(wo_all, layer_of(t - 1)))
                    last.then_inc(wo_psum, 1)
                if s2:
                    av(par, n, 3)
                for name, first, done in (("tq", 0, tq_psum), ("tk", P, tk_psum)):
                    if s1:
                        free(name, t, n)
                        for j in range(GC):
                            pe.wait_ge(qk_ready[j], n(1))
                            transpose(ring_bank(name)[:, cols(j)], qk[:, 1 - par, j, first:first + P],
                                      done if j == GC - 1 else None)

            run_steps(pe, step)

        @block.scalar
        def _(act):
            act.dma_start(gw_sb[:, :], gate).then_inc(d_params, 16)
            for dst, src in ((wqkv_all, wqkv), (wg_all, wg), (wo_all, wo), (w1_all, w1), (w2_all, w2)):
                act.dma_start(dst[:], src).then_inc(d_params, 16)
            act.dma_start(ln_sb[:], ln).then_inc(d_params, 16)
            act.dma_start(gn_sb[:], gn).then_inc(d_params, 16)
            act.dma_start(b1_sb[:], eb1).then_inc(d_params, 16)
            act.dma_start(ropec[:], rope_c).then_inc(d_params, 16)
            act.dma_start(ropes[:], rope_s).then_inc(d_params, 16)

            for g in range(NG):
                act.wait_ge(g_xT_psum, g + 1)
                act.copy(xnT[g % 2], bank[g % 2][:, :]).then_inc(g_xT_ready, 1)
                act.wait_ge(g_lT_psum, g + 1)
                act.copy(lT[g % 2], bank[2 + g % 2][0:E, :]).then_inc(g_lT_ready, 1)
            act.wait_ge(g_shifted, 1)
            act.activation(gt["exp"], gt["shifted"], ACT.Exp).then_inc(g_exp, 1)

            act.wait_ge(d_params, PARAMS)
            def expert(e, par, n):
                for f in range(FB):
                    b = row(b1_sb, e * FB + f)
                    need_alone(act, e_ha_psum[f], n(0))
                    act.activation(e_hT[:, f, 0:GT], bank[2 + f % 2][:, :], ACT.Gelu, bias=b).then_inc(e_ha_ready[f], 1)
                    need_alone(act, e_hb_psum[f], n(0))
                    act.activation(e_hT[:, f, GT:CAP], bank[4 + f % 2][:, 0:CAP - GT], ACT.Gelu,
                                   bias=b).then_inc(e_hb_ready[f], 1)

            run_experts(act, expert)

            def as_row(ap):
                return ap.unsqueeze(1)

            act.copy(wg_now[:, :], wg_all[:, 0, :]).then_inc(wg_ready, 1)

            def kv_copy(t, par, n, j):
                act.wait_ge(kvq_psum[j], n(1))
                src = bank[2 + j % 2][:, 2 * P:3 * P].rearrange("p (r w d) -> p r w d", r=4, w=2)
                act.copy(padded_heads(vpad[:, 1 - par, j, :]), src).then_inc(v_ready[j], 1)

            def step(t, par, n):
                s1, s2, s3, s4 = stages(t)
                if s1:
                    act.wait_ge(t1_psum, n(1))
                    act.activation(xT[:, :], ring_bank("t1")[:, :], ACT.Identity, bias=ln_sb[:, 1:2],
                                   scale=ln_sb[:, 0:1]).then_inc(xT_ready, 1)
                if s3:
                    act.wait_ge(var_psum, n(-1))
                    act.copy(var8[:, :], ring_bank("var")[0:H, :]).then_inc(var8_ready, 1)
                if s1:
                    act.wait_ge(g_psum, n(1))
                    i = (t + 1) % 4 if isinstance(t, int) else (t + 1) & 3
                    act.activation(row(gateT, i), as_row(ring_bank("g")[:, :]), ACT.Silu).then_inc(gate_ready, 1)
                    if not isinstance(t, int) or t + 2 < STEPS:
                        act.copy(as_row(wg_now[:, :]), row(wg_all, layer_of(t + 2))).then_inc(wg_ready, 1)
                    kv_copy(t, par, n, 0)
                if s4:
                    act.wait_ge(t2_psum, n(-2))
                    act.activation(x2T[:, :], ring_bank("t2")[:, :], ACT.Identity, bias=ln_sb[:, 1:2],
                                   scale=ln_sb[:, 0:1]).then_inc(x2T_ready, 1)
                if s1:
                    kv_copy(t, par, n, 1)
                if s4:
                    act.wait_ge(w1a_psum, n(-2))
                    act.activation(hT[:, 0, :], ring_bank("w1a")[:, :], ACT.Gelu_apprx_tanh).then_inc(ha_ready, 1)
                if s1:
                    kv_copy(t, par, n, 2)
                if s3:
                    act.wait_ge(rstd_ready, n(-1))
                    act.copy(rstdx[:, :].rearrange("p (h d) -> p h d", d=DH),
                             rstd[:, :].unsqueeze(2).to_broadcast([P, GC * H, DH])).then_inc(rstdx_ready, 1)
                if s4:
                    act.wait_ge(w1b_psum, n(-2))
                    act.activation(hT[:, 1, :], ring_bank("w1b")[:, :], ACT.Gelu_apprx_tanh).then_inc(hb_ready, 1)
                if not isinstance(t, int) or 0 <= t - 1 < STEPS:
                    act.copy(as_row(w1_now[:, :]), row(w1_all, layer_of(t - 1))).then_inc(w1_ready, 1)
                if s1:
                    kv_copy(t, par, n, 3)
                if s2:
                    act.wait_ge(av_done[GC - 1], n(0))
                    need(act, z1_ready, n(-1))
                    act.copy(ysb[:, :], bank[4][:, :])
                    act.activation(ysq[:, :], bank[4][:, :], ACT.Square).then_inc(y_ready, 1)
                if s1:
                    act.wait_ge(tq_psum, n(1))
                    for v in range(4):
                        act.activation(qT[:, 1 - par, v, :], ring_bank("tq")[:, :], ACT.Copy,
                                       scale=cst[:, HEADMASK + v:HEADMASK + v + 1])
                    act.copy(qT[:, 1 - par, 4, :], ring_bank("tq")[:, :]).then_inc(qT_ready, 1)
                    act.wait_ge(tk_psum, n(1))
                    act.copy(kT[:, 1 - par, :], ring_bank("tk")[:, :]).then_inc(kT_ready, 1)

            run_steps(act, step)

        @block.vector
        def _(dve):
            links = [0]

            def link(ins):
                links[0] += 1
                ins.then_inc(chained, 1)
                dve.wait_ge(chained, links[0])

            def tt(out, a, b, op):
                return nc.vector.tensor_tensor(out, a, b, op)

            for k in range(4):
                dve.wait_ge(d_x[k], 16)
                for c in range(8):
                    last = nc.vector.bn_stats(stats[:, c, :], xin[:, 8 * k + c, :])
                link(last)
                for c in range(8):
                    last = nc.vector.bn_aggr(mv0[:, 8 * k + c, :], stats[:, c, :])
                link(last)
                nc.vector.tensor_scalar(ve0[:, cols(k, 8)], mv0[:, cols(k, 8), 1], EPS, None, ALU.add).then_inc(ln0_var, 1)
            for k in range(4):
                dve.wait_ge(ln0_rstd, k + 1)
                for c in range(8 * k, 8 * k + 8):
                    last = nc.vector.tensor_scalar(res[:, c, :], xin[:, c, :], mv0[:, c, 0:1], rs0[:, c:c + 1],
                                                   ALU.subtract, ALU.mult)
                last.then_inc(ln0_done, 1)

            dve.wait_ge(d_params, PARAMS)
            dve.wait_ge(d_const, 16)
            wv = wqkv_all[:, :, 2 * P:3 * P].rearrange("p l (h d) -> p l h d", d=DH)
            mean = vare[:, :].rearrange("p (l h) -> p l h", l=L)
            link(nc.vector.tensor_reduce(mean, wv, AX.X, ALU.add))
            link(nc.vector.tensor_scalar(mean, mean, -1.0 / DH, None, ALU.mult))
            for l in range(L):
                last = tt(wv[:, l], wv[:, l], mean[:, l, :].unsqueeze(2).to_broadcast([P, H, DH]), ALU.add)
            link(last)

            def by_chunk(ap):
                return ap.rearrange("p (c e) -> p c e", e=E)

            def by_expert(ap):
                return ap.rearrange("p (e c) -> p c e", e=E)

            def over_e(ap):
                return ap.unsqueeze(2).to_broadcast([P, NCH, E])

            revexp = cst[:, REVEXP:REVEXP + E].unsqueeze(1).to_broadcast([P, NCH, E])
            dve.wait_ge(g_logits, 1)
            link(nc.vector.tensor_copy(gt["logit"], bank[4][:, 0:256]))
            link(nc.vector.tensor_reduce(gsm["max"][:, :], by_chunk(gt["logit"]), AX.X, ALU.max))
            tt(by_chunk(gt["shifted"]), by_chunk(gt["logit"]), over_e(gsm["max"][:, :]), ALU.subtract).then_inc(g_shifted, 1)
            link(tt(by_chunk(gt["equal"]), by_chunk(gt["logit"]), over_e(gsm["max"][:, :]), ALU.is_equal))
            link(tt(by_chunk(gt["score"]), by_chunk(gt["equal"]), revexp, ALU.mult))
            link(nc.vector.tensor_reduce(gsm["rev"][:, :], by_chunk(gt["score"]), AX.X, ALU.max))
            tt(by_expert(gt["onehot"]), revexp, over_e(gsm["rev"][:, :]), ALU.is_equal).then_inc(g_onehot, 1)
            dve.wait_ge(g_exp, 1)
            link(nc.vector.tensor_reduce(gsm["sum"][:, :], by_chunk(gt["exp"]), AX.X, ALU.add))
            link(nc.vector.reciprocal(gsm["inv"][:, :], gsm["sum"][:, :]))
            dve.wait_ge(g_ranks, 1)
            link(nc.vector.tensor_tensor_scan(gt["scan"], cst[:, NOTFIRST:NOTFIRST + 256], bank[6][:, 0:256], 0.0,
                                              ALU.mult, ALU.add))
            link(tt(gt["scan"], gt["scan"], bank[6][:, 0:256], ALU.subtract))
            link(tt(gt["rank"], gt["scan"], bank[5][:, 0:256], ALU.add))
            link(tt(g_prod, gt["rank"], gt["onehot"], ALU.mult))
            link(nc.vector.tensor_reduce(gsm["rank"][:, :], by_expert(g_prod), AX.X, ALU.add))
            link(nc.vector.tensor_scalar(gsm["kept"][:, :], gsm["rank"][:, :], float(CAP), None, ALU.is_le))
            tt(weight[:, :], gsm["inv"][:, :], gsm["kept"][:, :], ALU.mult)
            nc.vector.tensor_scalar(gsm["far"][:, :], gsm["kept"][:, :], -1e6, 1e6, ALU.mult, ALU.add)
            link(nc.vector.scalar_tensor_tensor(out=gsm["slot"][:, :], in0=gsm["rev"][:, :], scalar=-float(CAP),
                                                in1=gsm["rank"][:, :], op0=ALU.mult, op1=ALU.add))
            nc.vector.scalar_tensor_tensor(out=slots[:, :], in0=gsm["slot"][:, :], scalar=float(E * CAP - 1),
                                           in1=gsm["far"][:, :], op0=ALU.add, op1=ALU.add).then_inc(g_slots, 1)

            def expert(e, par, n):
                half = (e >> 1) if not isinstance(e, int) else e // 2
                def take(parity, k):
                    dve.wait_ge(e_rows_psum[0], k)
                    nc.vector.tensor_copy(e_xT[parity][:, 0:GT], bank[0][:, :]).then_inc(e_xT_ready[0], 1)
                    dve.wait_ge(e_rows_psum[1], k)
                    nc.vector.tensor_copy(e_xT[parity][:, GT:CAP], bank[1][:, 0:CAP - GT]).then_inc(e_xT_ready[1], 1)

                if isinstance(e, int) and e == 0:
                    take(0, 1)
                if not (isinstance(e, int) and e == E - 1):
                    take(1 - par, n(1))
                dve.wait_ge(d_ew[par], (half + 1) * 48)
                dve.wait_ge(d_ey[par], half * 32) if not isinstance(half, int) or half > 0 else None
                dve.wait_ge(e_y_psum[0], n(0))
                tt(e_y[par][:, 0:GC, :], bank[6][:, :].rearrange("p (i d) -> p i d", d=D),
                   e_b2[par].unsqueeze(1).to_broadcast([P, GC, D]), ALU.add).then_inc(e_y_ready[0], 1)
                dve.wait_ge(e_y_psum[1], n(0))
                tt(e_y[par][:, GC, :], bank[7][:, 0:P], e_b2[par], ALU.add)
                tt(e_y[par][0:1, FULL, :], bank[7][0:1, P:2 * P], e_b2[par][0:1, :], ALU.add).then_inc(e_y_ready[1], 1)

            run_experts(dve, expert)

            for q in range(2):
                nc.vector.memset(bank[q][:, :], 0.0)
            nc.vector.memset(state[:, :], 0.0).then_inc(prepared, 1)
            dve.wait_ge(prepared, 1)

            def ln_apply(i, mv, rs, dst, done):
                x = group_rows(res, i)
                for j in range(GC):
                    last = nc.vector.tensor_scalar(dst[:, j, :], x[:, j, :], mv[:, j, 0:1], rs[:, j:j + 1],
                                                   ALU.subtract, ALU.mult)
                last.then_inc(done, 1)

            def probs_of(n, j):
                dve.wait_ge(att_psum[j], n(0))
                need(dve, av_done[(j + 2) % GC], n(0) if j >= 2 else n(-1))
                for q in range(2):
                    last = tt(probs[:, j % 2, q, :].rearrange("p (v n) -> p v n", v=4),
                              bank[q][:, :].rearrange("p (v n) -> p v n", v=4),
                              tri.unsqueeze(1).to_broadcast([P, 4, P]), ALU.mult)
                last.then_inc(probs_ready[j], 1)

            def chunk(t, par, n, j, s1, s2):
                b = bank[2 + j % 2]
                g = group_of(t) & (GC - 1) if s2 else 0
                if s2:
                    need(dve, state_ready[(j + 3) % GC], n(0) if j else n(-1))
                    keep = row(cst, (g + KEEP)) if j == 0 else 1.0
                    nc.vector.scalar_tensor_tensor(out=smask[:, j % 2, :], in0=state[:, :], scalar=keep,
                                                   in1=blockdec, op0=ALU.mult, op1=ALU.mult).then_inc(smask_ready[j], 1)
                dve.wait_ge(v_ready[j] if s1 else kvq_psum[j], n(1))
                if s2:
                    keep = row(cst, (g + DECKEEP)) if j == 0 else cst[:, DECAY:DECAY + 1]
                    last = nc.vector.scalar_tensor_tensor(out=state[:, :], in0=state[:, :], scalar=keep,
                                                          in1=b[:, 3 * P:4 * P], op0=ALU.mult, op1=ALU.add)
                    last.then_inc(state_ready[j], 1)
                if s1:
                    need(dve, qk_ready[(j + 2) % GC], n(1) if j >= 2 else n(0))
                    src = b[:, 0:2 * P]
                    tt(rc[:, j % 2:j % 2 + 1, :], src.unsqueeze(1), chunk_row(ropec, t + 1, j), ALU.mult)

                    def pairs(ap):
                        return ap.rearrange("p a (h s d) -> p (a h) s d", s=2, d=DH // 2)

                    tt(pairs(rs_[:, j % 2:j % 2 + 1, :]), pairs(src.unsqueeze(1))[:, :, ::-1, :],
                       pairs(chunk_row(ropes, t + 1, j)), ALU.mult).then_inc(kvq_read[j], 1)
                else:
                    nc.vector.engine_nop().then_inc(kvq_read[j], 1)

            ln1 = (stats[:, 0:GC], mv1, ve1, ln1_st, ln1_mv, ln1_var)
            ln2 = (stats[:, GC:2 * GC], mv2, ve2, ln2_st, ln2_mv, ln2_var)

            def ln_stats(i, which, value):
                st, mv, ve, stat_done, mean_done, var_done = which
                x = group_rows(res, i)
                for j in range(GC):
                    last = nc.vector.bn_stats(st[:, j, :], x[:, j, :])
                last.then_inc(stat_done, 1)
                need_alone(dve, stat_done, value)
                for j in range(GC):
                    last = nc.vector.bn_aggr(mv[:, j, :], st[:, j, :])
                last.then_inc(mean_done, 1)
                dve.wait_ge(mean_done, value)
                nc.vector.tensor_scalar(ve[:, :], mv[:, :, 1], EPS, None, ALU.add).then_inc(var_done, 1)

            ln_stats(0, ln1, 1)
            dve.wait_ge(ln1_rstd, 1)
            ln_apply(0, mv1, rs1, xhat, xhat_ready)

            def step(t, par, n):
                s1, s2, s3, s4 = stages(t)
                s0 = not isinstance(t, int) or t + 2 < STEPS
                if s2:
                    probs_of(n, 0)
                if s4:
                    dve.wait_ge(ln2_rstd, n(-2))
                    need(dve, t2_psum, n(-3))
                    ln_apply(t - 2, mv2, rs2, xhat2, x2hat_ready)
                if s1 or s2:
                    chunk(t, par, n, 0, s1, s2)
                if s2:
                    probs_of(n, 1)
                if s3:
                    dve.wait_ge(vt_psum, n(-1))
                    nc.vector.tensor_scalar(vare[:, :], ring_bank("vt")[:, 0:GC * H], EPS, None,
                                            ALU.add).then_inc(vare_ready, 1)
                if s1 or s2:
                    chunk(t, par, n, 1, s1, s2)
                if s2:
                    probs_of(n, 2)
                if s1 or s2:
                    chunk(t, par, n, 2, s1, s2)
                if s3:
                    dve.wait_ge(rt_psum, n(-1))
                    l = layer_of(t - 1)
                    nc.vector.scalar_tensor_tensor(out=z1[:, :], in0=ring_bank("rt")[:, :], scalar=row(gn_sb, l),
                                                   in1=ysb[:, :], op0=ALU.mult, op1=ALU.mult).then_inc(z1_ready, 1)
                    dve.wait_ge(z1_ready, n(-1))
                    i = (t - 1) % 4 if isinstance(t, int) else (t - 1) & 3
                    nc.vector.scalar_tensor_tensor(out=zT[:, :].unsqueeze(1), in0=z1[:, :].unsqueeze(1),
                                                   scalar=row(gn_sb, l + L), in1=row(gateT, i), op0=ALU.add,
                                                   op1=ALU.mult).then_inc(zT_ready, 1)
                if s2:
                    probs_of(n, 3)
                if s1 or s2:
                    chunk(t, par, n, 3, s1, s2)
                if s4:
                    dve.wait_ge(w2_psum, n(-2))
                    x = group_rows(res, t - 2)
                    tt(x, x, ring_bank("w2")[:, :].rearrange("p (j d) -> p j d", d=D), ALU.add).then_inc(ffn_added, 1)
                if s0:
                    ln_stats(t + 2, ln1, n(2))
                if s3:
                    dve.wait_ge(wo_psum, n(-1))
                    x = group_rows(res, t - 1)
                    tt(x, x, ring_bank("wo")[:, :].rearrange("p (j d) -> p j d", d=D), ALU.add).then_inc(attn_added, 1)
                    need_alone(dve, attn_added, n(-1))
                    ln_stats(t - 1, ln2, n(-1))
                if s0:
                    dve.wait_ge(ln1_rstd, n(2))
                    need(dve, t1_psum, n(1))
                    ln_apply(t + 2, mv1, rs1, xhat, xhat_ready)

            run_steps(dve, step)

            dve.wait_ge(d_gather, 16 * NCH)
            dve.wait_ge(ffn_added, STEPS)
            for g in range(NG):
                x = xin[:, cols(g, GC), :]
                tt(x, x, res[:, cols(g, GC), :], ALU.add).then_inc(summed, 1)
                dve.wait_ge(summed, g + 1)
                for c in range(GC * g, GC * g + GC):
                    last = nc.vector.scalar_tensor_tensor(out=xin[:, c, :], in0=routed[:, c, :], scalar=weight[:, c:c + 1],
                                                          in1=xin[:, c, :], op0=ALU.mult, op1=ALU.add)
                last.then_inc(out_ready, 1)

        @block.gpsimd
        def _(pool):
            nc.gpsimd.memset(zeros[:, :], 0.0).then_inc(zeroed, 1)
            nc.gpsimd.memset(power[:, :], -0.5).then_inc(cleared, 1)
            nc.gpsimd.memset(flat(routed[:, :, :]), 0.0).then_inc(cleared, 1)
            pool.wait_ge(cleared, 2)

            def reciprocal_root(out, v):
                return nc.gpsimd.tensor_tensor(out, v, power[:, 0:v.shape[1]], ALU.pow)

            for k in range(4):
                pool.wait_ge(ln0_var, k + 1)
                reciprocal_root(rs0[:, cols(k, 8)], ve0[:, cols(k, 8)]).then_inc(ln0_rstd, 1)

            pool.wait_ge(g_slots, 1)
            pool.wait_ge(ln0_done, 4)
            pool.wait_ge(d_zero, 16 * (E * D // P))
            for c in range(NCH):
                nc.gpsimd.indirect_dma_start(
                    out=slot_x, out_offset=bass.IndirectOffsetOnAxis(ap=slots[:, c:c + 1], axis=0),
                    in_=res[:, c, :], in_offset=None, bounds_check=E * CAP - 1, oob_is_err=False).then_inc(d_scatter, 16)

            slot_tiles = slot_y.rearrange("(e r) d -> e r d", e=E)

            def expert(e, par, n):
                dst = slot_tiles[e:e + 1] if isinstance(e, int) else slot_tiles[bass.ds(e, 1)]
                pool.wait_ge(e_y_ready[1], n(0))
                pool.dma_start(dst[:, 0:FULL * P, :].rearrange("a (i p) d -> p (a i) d", p=P),
                               e_y[par][:, 0:FULL, :]).then_inc(d_ey[par], 16)
                pool.dma_start(dst[:, FULL * P:CAP, :].rearrange("a r d -> (a r) d"),
                               e_y[par][0:1, FULL, :]).then_inc(d_ey[par], 16)

            run_experts(pool, expert)

            for k in range(2):
                pool.wait_ge(d_ey[k], 32 * (E // 2))
            nc.gpsimd.memset(vpad[:].rearrange("p a b c -> p (a b c)"), 0.0).then_inc(cleared, 1)
            for c in range(NCH):
                nc.gpsimd.indirect_dma_start(
                    out=routed[:, c, :], out_offset=None, in_=slot_y,
                    in_offset=bass.IndirectOffsetOnAxis(ap=slots[:, c:c + 1], axis=0),
                    bounds_check=E * CAP - 1, oob_is_err=False).then_inc(d_gather, 16)

            pool.wait_ge(ln1_var, 1)
            reciprocal_root(rs1[:, :], ve1[:, :]).then_inc(ln1_rstd, 1)

            def rotated(par, n, j):
                pool.wait_ge(kvq_read[j], n(1))
                nc.gpsimd.tensor_tensor(qk[:, 1 - par, j, :], rc[:, j % 2, :], rs_[:, j % 2, :], ALU.add).then_inc(qk_ready[j], 1)

            def step(t, par, n):
                s1, s2, s3, s4 = stages(t)
                if s1:
                    rotated(par, n, 0)
                if s3:
                    pool.wait_ge(vare_ready, n(-1))
                    reciprocal_root(rstd[:, :], vare[:, :]).then_inc(rstd_ready, 1)
                if s1:
                    rotated(par, n, 1)
                    rotated(par, n, 2)
                    rotated(par, n, 3)
                if not isinstance(t, int) or t + 2 < STEPS:
                    pool.wait_ge(ln1_var, n(2))
                    reciprocal_root(rs1[:, :], ve1[:, :]).then_inc(ln1_rstd, 1)
                if s3:
                    pool.wait_ge(ln2_var, n(-1))
                    reciprocal_root(rs2[:, :], ve2[:, :]).then_inc(ln2_rstd, 1)

            run_steps(pool, step)


def kernel(**inputs):
    import concourse.bacc as _bacc
    from concourse.bass_utils import run_bass_kernel_spmd as _run

    a = {k: np.asarray(v) for k, v in inputs.items()}
    B, S, D = a["L0_attn_X"].shape
    H, DH = 8, 16
    order = np.arange(D).reshape(H, DH // 2, 2).transpose(0, 2, 1).reshape(D)
    qkv = [a["L0_attn_Wq"][:, :, order], a["L0_attn_Wk"][:, :, order], a["L0_attn_Wv"]]
    L, F = a["L0_attn_W1"].shape[0], a["L0_attn_W1"].shape[2]
    consts, rope_c, rope_s = shape_constants(S, H, DH)
    arrays = {
        "x": a["L0_attn_X"].reshape(B * S, D),
        "wqkv": np.concatenate(qkv, axis=2).transpose(1, 0, 2),
        "wg": a["L0_attn_Wg"].transpose(1, 0, 2),
        "wo": a["L0_attn_Wo"].transpose(1, 0, 2),
        "w1": a["L0_attn_W1"].transpose(1, 0, 2),
        "w2": a["L0_attn_W2"].reshape(L, F // P, P, D).transpose(2, 0, 1, 3).reshape(P, L, (F // P) * D),
        "ln": np.stack([a["L0_attn_ln_scale"], a["L0_attn_ln_bias"]], axis=1),
        "gn": np.concatenate([a["L0_attn_gn_scale"], a["L0_attn_gn_bias"]], axis=0).T,
        "gate": a["L0_ffn_wg"],
        "ew1": a["L0_ffn_W1"],
        "eb1": a["L0_ffn_b1"].reshape(a["L0_ffn_b1"].shape[0], -1, P).transpose(2, 0, 1).reshape(P, -1),
        "ew2": a["L0_ffn_W2"],
        "eb2": a["L0_ffn_b2"],
        "consts": consts,
        "rope_c": rope_c,
        "rope_s": rope_s,
    }
    arrays = {f"in_{k}": np.ascontiguousarray(v) for k, v in arrays.items()}
    nc = _bacc.Bacc("TRN2", target_bir_lowering=False, num_devices=1)
    args = [nc.dram_tensor(k, v.shape, mybir.dt.from_np(v.dtype), kind="ExternalInput").ap() for k, v in arrays.items()]
    args.append(nc.dram_tensor("out_0", (B * S, D), F32, kind="ExternalOutput").ap())
    retention_moe(nc, *args)
    r = _run(nc, [arrays], core_ids=[0])
    return r.results[0]["out_0"].reshape(B, S, D)
```

```python
from contextlib import ExitStack

import numpy as np

import concourse.bass as bass
from concourse import mybir
from concourse.alu_op_type import AluOpType as ALU

F32 = mybir.dt.float32
I32 = mybir.dt.int32
U32 = mybir.dt.uint32
ACT = mybir.ActivationFunctionType
AX = mybir.AxisListType

P = 128
GC = 4
GT = GC * P
HP = P // 2
EPS = 1e-5

IDENT = 0
TRI = IDENT + P
CAUSAL = TRI + P
ONES = CAUSAL + HP
BLOCKDEC = ONES + P
HEADMASK = BLOCKDEC + P
BLOCKMEAN = HEADMASK + 4
DECAY = BLOCKMEAN + 8
KEEP = DECAY + 1
DECKEEP = KEEP + 4
REVEXP = DECKEEP + 4
NOTFIRST = REVEXP + 8
CONSTS = NOTFIRST + 8 * 32


def shape_constants(S, H, DH):
    D = H * DH
    half = DH // 2
    f32 = np.float32
    ends = np.log(1 / 32), np.log(1 / 64)
    gam = (1.0 - np.exp(np.linspace(ends[0], ends[1], H).astype(f32))).astype(f32)
    lg = np.log(gam).astype(f32).astype(np.float64)
    inv = (f32(1.0) / np.power(f32(10000.0), np.arange(0, DH, 2, dtype=f32) / f32(DH))).astype(f32)
    ang = (np.arange(S, dtype=f32)[:, None] * inv[None, :]).astype(f32).astype(np.float64)
    cos, sin = np.cos(ang), np.sin(ang)
    within = np.arange(S) % HP
    qd = np.exp(within[:, None] * lg)
    kd = np.exp(-within[:, None] * lg)

    def table(first, second, decay):
        t = np.concatenate([first, second], axis=1)[:, None, :] * decay[:, :, None]
        return t.reshape(S, D)

    rope_c = np.concatenate([table(cos, cos, qd), table(cos, cos, kd)], axis=1)
    rope_s = np.concatenate([table(-sin, sin, qd), table(sin, -sin, kd)], axis=1)
    rope_c, rope_s = (
        np.ascontiguousarray(t.reshape(S // P, P, 2 * D).transpose(1, 0, 2)).astype(f32)
        for t in (rope_c, rope_s)
    )
    c = np.zeros((P, CONSTS), f32)
    feat = np.arange(P) // DH
    dec = np.exp(HP * lg)[feat]
    c[:, IDENT:IDENT + P] = np.eye(P)
    c[:, TRI:TRI + P] = np.triu(np.ones((P, P)))
    c[:, CAUSAL:CAUSAL + HP] = np.tile(np.triu(np.ones((HP, HP))), (2, 1))
    c[:, ONES:ONES + P] = 1.0
    c[:, BLOCKDEC:BLOCKDEC + P] = (feat[:, None] == feat[None, :]) * dec[:, None]
    for v in range(4):
        c[:, HEADMASK + v] = feat % 4 == v
    for h in range(H):
        c[:, BLOCKMEAN + h] = (feat == h) / DH
    c[:, DECAY] = dec
    for g in range(4):
        c[:, KEEP + g] = g > 0
        c[:, DECKEEP + g] = dec * (g > 0)
    c[:, REVEXP:REVEXP + 8] = 8 - np.arange(8)
    c[:, NOTFIRST:] = np.tile(np.arange(32) > 0, 8)
    return c, rope_c, rope_s


def retention_moe(nc, x, wqkv, wg, wo, w1, w2, ln, gn, gate, ew1, eb1, ew2, eb2,
                  consts, rope_c, rope_s, out):
    NTOK, D = x.shape
    NCH = NTOK // P
    NG = NCH // GC
    SCH = rope_c.shape[1]
    L = wo.shape[1]
    H, DH = 8, 16
    E, _, FE = ew1.shape
    FB = FE // P
    CAP = int(NTOK / E * 1.25) + 1
    FULL = CAP // P
    TAIL = CAP - FULL * P
    assert D == P and TAIL == 1 and FULL == 5 and NG == 8 and L == 4
    STEPS = L * NG
    PARAMS = 16 * 8
    FIRST_GROUPS = ((0, 1, 2), (3, 4, 5), (6, 7))
    LAST_GROUPS = ((0, 1), (2, 3, 4), (5, 6, 7))

    with ExitStack() as ctx:
        def sb(name, shape, dt=F32):
            return ctx.enter_context(nc.sbuf_tensor(name, shape, dt))

        def sem(name):
            return ctx.enter_context(nc.semaphore(name))

        def sems(name, n):
            return [sem(f"{name}{i}") for i in range(n)]

        bank = [ctx.enter_context(nc.psum_tensor(f"bank{i}", [P, 512], F32)) for i in range(8)]

        cst = sb("cst", [P, CONSTS])
        ident, tri, ones = (cst[:, o:o + P] for o in (IDENT, TRI, ONES))
        causal = cst[:, CAUSAL:CAUSAL + HP]
        blockdec = cst[:, BLOCKDEC:BLOCKDEC + P]
        blockmean = cst[:, BLOCKMEAN:BLOCKMEAN + H]
        xin = sb("xin", [P, NCH, D])
        res = sb("res", [P, NCH, D])
        ropec = sb("ropec", [P, SCH, 2 * D])
        ropes = sb("ropes", [P, SCH, 2 * D])
        wqkv_all = sb("wqkv_all", [P, L, 3 * D])
        wg_all = sb("wg_all", [P, L, D])
        wo_all = sb("wo_all", [P, L, D])
        w1_all = sb("w1_all", [P, L, 2 * D])
        w2_all = sb("w2_all", [P, L, 2 * D])
        ln_sb = sb("ln_sb", [P, 2])
        gn_sb = sb("gn_sb", [P, 2 * L])
        power = sb("power", [P, 32])
        stats = sb("stats", [P, 8, 6])
        weight = sb("weight", [P, NCH])
        slots = sb("slots", [P, NCH], U32)

        xhat = sb("xhat", [P, GC, D])
        xT = sb("xT", [P, GT])
        xhat2 = sb("xhat2", [P, GC, D])
        x2T = sb("x2T", [P, GT])
        wg_now = sb("wg_now", [P, D])
        w1_now = sb("w1_now", [P, 2 * D])
        gateT = sb("gateT", [P, 4, GT])
        rc = sb("rc", [P, 2, 2 * D])
        rs_ = sb("rs_", [P, 2, 2 * D])
        qk = sb("qk", [P, 2, GC, 2 * D])
        vpad = sb("vpad", [P, 2, GC, 2 * D])
        qT = sb("qT", [P, 2, 5, GT])
        kT = sb("kT", [P, 2, GT])
        probs = sb("probs", [P, 2, 2, 4 * HP])
        state = sb("state", [P, 2, D])
        smask = sb("smask", [P, 4, D])
        ysb = sb("ysb", [P, GT])
        ysq = sb("ysq", [P, GT])
        var8 = sb("var8", [H, GT])
        vare = sb("vare", [P, GC * H])
        rstd = sb("rstd", [P, GC * H])
        rstdx = sb("rstdx", [P, GT])
        zT = sb("zT", [P, GT])
        hT = sb("hT", [P, 2, GT])
        mv1 = sb("mv1", [P, GC, 2])
        ve1 = sb("ve1", [P, GC])
        rs1 = sb("rs1", [P, GC])
        mv2 = sb("mv2", [P, GC, 2])
        ve2 = sb("ve2", [P, GC])
        rs2 = sb("rs2", [P, GC])

        gw_sb = sb("gw_sb", [P, E])
        b1_sb = sb("b1_sb", [P, E * FB])
        mv0 = sb("mv0", [P, NCH, 2])
        ve0 = sb("ve0", [P, NCH])
        rs0 = sb("rs0", [P, NCH])
        gsm = {n: sb("g_" + n, [P, NCH]) for n in ("max", "sum", "inv", "rev", "rank", "kept", "slot", "far")}
        e_hT = sb("e_hT", [P, FB, CAP])
        zeros = e_hT[:, 0, :]
        e_room = sb("e_room", [P, 26 * 256 + 2])

        def room(at, *shape):
            n = int(np.prod(shape))
            ap = e_room[:, at * 256:at * 256 + n]
            return ap if len(shape) == 1 else ap.rearrange("p (a b) -> p a b", b=shape[1])

        e_w1 = [room(2 * k, GT) for k in range(2)]
        e_w2 = [room(4 + 2 * k, FB, D) for k in range(2)]
        e_x = [room(8 + 3 * k, FULL + 1, D) for k in range(2)]
        e_y = [room(14 + 3 * k, FULL + 1, D) for k in range(2)]
        e_b2 = [e_room[:, 20 * 256 + D * k:20 * 256 + D * (k + 1)] for k in range(2)]
        e_xT = [e_room[:, 21 * 256 + CAP * k:21 * 256 + CAP * (k + 1)] for k in range(2)]
        routed = room(0, NCH, D)
        gt = {n: room(8 + i, 256) for i, n in enumerate(
            ("logit", "shifted", "exp", "equal", "score", "onehot", "scan", "rank"))}
        g_prod = room(16, 256)
        xnT = [room(17 + 2 * k, GT) for k in range(2)]
        lT = [room(21 + 2 * k, GT)[0:E, :] for k in range(2)]

        slot_x = nc.dram_tensor("slot_x", [E * CAP, D], F32, kind="Internal").ap()
        slot_y = nc.dram_tensor("slot_y", [E * CAP, D], F32, kind="Internal").ap()
        x_dram = x.rearrange("(c p) d -> p c d", p=P)
        out_dram = out.rearrange("(c p) d -> p c d", p=P)

        d_const, d_gate, d_params, d_zero = (sem(n) for n in ("d_const", "d_gate", "d_params", "d_zero"))
        d_rope = sems("d_rope", 2)
        d_scatter, d_gather = sems("d_scatter", len(FIRST_GROUPS)), sems("d_gather", len(LAST_GROUPS))
        d_x = sems("d_x", 4)
        d_ew, d_ex, d_ey = sems("d_ew", 2), sems("d_ex", 2), sems("d_ey", 2)
        d_out = sem("d_out")
        zeroed, cleared, v_centred, prepared, ln0_var, ln0_rstd, ln0_done = (
            sem(n) for n in ("zeroed", "cleared", "v_centred", "prepared", "ln0_var", "ln0_rstd", "ln0_done"))
        g_xT_psum, g_xT_ready, g_lT_psum, g_lT_ready, g_logits, g_shifted, g_exp, g_onehot, g_ranks, g_slots, \
            chained = (sem(n) for n in ("g_xT_psum", "g_xT_ready", "g_lT_psum", "g_lT_ready", "g_logits",
                                        "g_shifted", "g_exp", "g_onehot", "g_ranks", "g_slots", "chained"))
        e_rows_psum, e_xT_ready, e_y_psum, e_y_ready = (
            sems(n, 2) for n in ("e_rows_psum", "e_xT_ready", "e_y_psum", "e_y_ready"))
        e_ha_psum, e_hb_psum, e_ha_ready, e_hb_ready = (
            sems(n, FB) for n in ("e_ha_psum", "e_hb_psum", "e_ha_ready", "e_hb_ready"))
        t1_psum, t2_psum, var_psum, g_psum, vt_psum, w1a_psum, w1b_psum, rt_psum, w2_psum, wo_psum, \
            tq_psum, tk_psum, y_psum = (sem(n + "_psum") for n in (
                "t1", "t2", "var", "g", "vt", "w1a", "w1b", "rt", "w2", "wo", "tq", "tk", "y"))
        xhat_ready, xT_ready, x2hat_ready, x2T_ready, var8_ready, gate_ready, vare_ready, rstd_ready, \
            ha_ready, hb_ready, z1_ready, zT_ready, ffn_added, attn_added, q_ready, qa_ready, qb_ready, kT_ready, y_ready, \
            wg_ready, w1_ready, ln1_var, ln1_rstd, ln2_var, ln2_rstd, ln1_st, ln2_st, ln1_mv, ln2_mv, rstdx_ready = (sem(n) for n in (
                "xhat_ready", "xT_ready", "x2hat_ready", "x2T_ready", "var8_ready", "gate_ready", "vare_ready",
                "rstd_ready", "ha_ready", "hb_ready", "z1_ready", "zT_ready", "ffn_added", "attn_added",
                "q_ready", "qa_ready", "qb_ready", "kT_ready", "y_ready", "wg_ready", "w1_ready", "ln1_var", "ln1_rstd", "ln2_var",
                "ln2_rstd", "ln1_st", "ln2_st", "ln1_mv", "ln2_mv", "rstdx_ready"))
        scores_psum, probs_ready, av_done, qkv_psum, smask_ready, half_ready, state_ready, qkv_read, qk_ready = (
            sems(n, GC) for n in ("scores_psum", "probs_ready", "av_done", "qkv_psum", "smask_ready",
                                  "half_ready", "state_ready", "qkv_read", "qk_ready"))
        passed = {e: sem(f"passed_{e.value}") for e in (nc.tensor.engine, nc.scalar.engine, nc.vector.engine)}
        summed, out_ready = sem("summed"), sem("out_ready")

        USES = [
            ("t1", 1, xT_ready), ("var", -1, var8_ready), ("g", 1, gate_ready), ("vt", -1, vare_ready),
            ("t2", -2, x2T_ready), ("w1a", -2, ha_ready), ("w1b", -2, hb_ready), ("rt", -1, z1_ready),
            ("w2", -2, ffn_added), ("tq", 1, q_ready), ("tk", 1, kT_ready), ("wo", -1, attn_added),
        ]
        PLACE = {name: i for i, (name, _, _) in enumerate(USES)}

        def ring_bank(name):
            return bank[5 + PLACE[name] % 3]

        def before(name, t):
            k = PLACE[name] - 3
            while True:
                who, off, s = USES[k % len(USES)]
                off += k // len(USES)
                if not isinstance(t, int):
                    return s, off
                if k // len(USES) + t < -1:
                    return None
                if 0 <= t + off < STEPS:
                    return s, off
                k -= 3

        class Counts:

            def __init__(self, eng, t):
                self.t, self.fixed = t, isinstance(t, int)
                self.reg = None if self.fixed else {k: eng.snap(t + (k + 1)) for k in range(-2, 3)}

            def __call__(self, k):
                return self.t + k + 1 if self.fixed else self.reg[k]

        def need(eng, s, value):
            if not isinstance(value, int) or value > 0:
                eng.wait_ge(s, value)

        def need_alone(eng, s, value):
            need(eng, s, value)
            if not isinstance(value, int):
                eng.sem_inc(passed[eng.engine], 1)

        def stages(t):
            if not isinstance(t, int):
                return True, True, True, True
            return tuple(0 <= t + k < STEPS for k in (1, 0, -1, -2))

        FIRST, LAST = 2, STEPS - 3
        UNROLL = 4
        assert (LAST - FIRST + 1) % UNROLL == 0

        def run_steps(eng, step, experts):
            for t in range(-1, FIRST):
                step(t, t % 2, Counts(eng, t))
            experts()
            with eng.Fori(0, (LAST - FIRST + 1) // UNROLL) as i:
                for k in range(UNROLL):
                    t = i * UNROLL + (FIRST + k)
                    step(t, (FIRST + k) % 2, Counts(eng, t))
            for t in range(LAST + 1, STEPS + 2):
                step(t, t % 2, Counts(eng, t))

        def run_experts(eng, expert):
            for e in (0, 1):
                expert(e, e, Counts(eng, e))
            with eng.Fori(0, (E - 4) // 2) as i:
                for k in range(2):
                    e = i * 2 + (2 + k)
                    expert(e, k, Counts(eng, e))
            for e in (E - 2, E - 1):
                expert(e, e % 2, Counts(eng, e))

        def layer_of(i):
            return (i // NG) if isinstance(i, int) else (i >> 3) & (L - 1)

        def group_of(i):
            return i % NG if isinstance(i, int) else i & (NG - 1)

        def row(ap, i):
            return ap[:, i:i + 1] if isinstance(i, int) else ap[:, bass.ds(i, 1)]

        def group_rows(ap, i):
            g = group_of(i)
            if isinstance(g, int):
                return ap[:, GC * g:GC * g + GC, :]
            return ap[:, bass.ds(g * GC, GC), :]

        def chunk_row(ap, i, j):
            c = (group_of(i) & (ap.shape[1] // GC - 1)) * GC + j
            return row(ap, c)

        def cols(j, n=P):
            return slice(n * j, n * j + n)

        def flat(ap):
            return ap.rearrange("p a b -> p (a b)")

        def padded_heads(ap):
            return ap.rearrange("p (r w d) -> p r w d", r=4, d=DH)[:, :, 0:4:3, :]

        block = ctx.enter_context(nc.Block())

        @block.sync
        def _(sp):
            sp.dma_start(cst[:], consts).then_inc(d_const, 16)
            for k in range(4):
                sp.dma_start(xin[:, cols(k, 8), :], x_dram[:, cols(k, 8), :]).then_inc(d_x[k], 16)
            sp.wait_ge(zeroed, 1)
            slot_rows = slot_x.rearrange("r d -> (r d)").rearrange("(p k) -> p k", p=P)
            for k in range(E * CAP * D // P // CAP):
                sp.dma_start(slot_rows[:, cols(k, CAP)], zeros[:, :]).then_inc(d_zero, 16)

            def load_weights(e, par):
                a = ew1[bass.ds(e, 1)] if not isinstance(e, int) else ew1[e:e + 1]
                b = ew2[bass.ds(e, 1)] if not isinstance(e, int) else ew2[e:e + 1]
                d = eb2[bass.ds(e, 1)] if not isinstance(e, int) else eb2[e:e + 1]
                sp.dma_start(e_w1[par], a.rearrange("a p f -> (a p) f")).then_inc(d_ew[par], 16)
                sp.dma_start(e_w2[par], b.rearrange("a (f p) d -> p (a f) d", p=P)).then_inc(d_ew[par], 16)
                sp.dma_start(e_b2[par], d.rearrange("a d -> (a d)").partition_broadcast(P)).then_inc(d_ew[par], 16)

            slot_tiles = slot_x.rearrange("(e r) d -> e r d", e=E)

            def load_rows(e, par):
                src = slot_tiles[e:e + 1] if isinstance(e, int) else slot_tiles[bass.ds(e, 1)]
                sp.dma_start(e_x[par][:, 0:FULL, :], src[:, 0:FULL * P, :].rearrange(
                    "a (i p) d -> p (a i) d", p=P)).then_inc(d_ex[par], 16)
                sp.dma_start(e_x[par][0:1, FULL, :], src[:, FULL * P:CAP, :].rearrange(
                    "a r d -> (a r) d")).then_inc(d_ex[par], 16)

            for k, groups in enumerate(FIRST_GROUPS):
                sp.wait_ge(d_scatter[k], len(groups) * 16 * GC)
            load_weights(0, 0)
            load_weights(1, 1)
            load_rows(0, 0)
            load_rows(1, 1)
            with sp.Fori(0, (E - 2) // 2) as i:
                for k in range(2):
                    e = i * 2 + k
                    sp.wait_ge(e_y_ready[1], e + 1)
                    load_weights(e + 2, k)
                    load_rows(e + 2, k)

            for g in range(NG):
                sp.wait_ge(out_ready, g + 1)
                sp.dma_start(out_dram[:, cols(g, GC), :], xin[:, cols(g, GC), :]).then_inc(d_out, 16)
            sp.wait_ge(d_out, 16 * NG)

        @block.tensor
        def _(pe):
            def transpose(dst, src, last=None):
                mm = pe.transpose(dst, src, ident[0:src.shape[0], 0:src.shape[0]])
                if last is not None:
                    mm.then_inc(last, 1)

            def mm(dst, lhsT, rhs, start=True, stop=True):
                return pe.matmul(dst, lhsT, rhs, start=start, stop=stop)

            pe.wait_ge(d_const, 16)
            for i in range(NG + 2):
                g = i
                if g < NG:
                    if g % 2 == 0:
                        pe.wait_ge(ln0_done, g // 2 + 1)
                    if g >= 2:
                        pe.wait_ge(g_xT_ready, g - 1)
                    for j in range(GC):
                        transpose(bank[g % 2][:, cols(j)], res[:, GC * g + j, :], g_xT_psum if j == GC - 1 else None)
                g = i - 1
                if 0 <= g < NG:
                    if g == 0:
                        pe.wait_ge(d_gate, 16)
                    pe.wait_ge(g_xT_ready, g + 1)
                    if g >= 2:
                        pe.wait_ge(g_lT_ready, g - 1)
                    mm(bank[2 + g % 2][0:E, :], gw_sb[:, :], xnT[g % 2]).then_inc(g_lT_psum, 1)
                g = i - 2
                if g >= 0:
                    pe.wait_ge(g_lT_ready, g + 1)
                    for j in range(GC):
                        c = GC * g + j
                        transpose(bank[4][:, cols(c, E)], lT[g % 2][:, cols(j)], g_logits if c == NCH - 1 else None)
            pe.wait_ge(g_onehot, 1)
            mm(bank[0][:, 0:256], tri, gt["onehot"])
            mm(bank[1][:, 0:256], ones, gt["onehot"]).then_inc(g_ranks, 1)

            def expert(e, par, n):
                def rows(x, parity, k):
                    pe.wait_ge(d_ex[parity], k)
                    for i in range(GC):
                        transpose(bank[0][:, cols(i)], x[:, i, :], e_rows_psum[0] if i == GC - 1 else None)
                    transpose(bank[1][:, 0:P], x[:, GC, :])
                    mm(bank[1][:, P:P + 1], x[0:1, FULL, :], ones[0:1, 0:1]).then_inc(e_rows_psum[1], 1)

                first = isinstance(e, int) and e == 0
                final = isinstance(e, int) and e == E - 1
                half = (e >> 1) if not isinstance(e, int) else e // 2
                if first:
                    rows(e_x[0], 0, 32)
                pe.wait_ge(d_ew[par], (half + 1) * 48)
                for f in range(FB):
                    w = e_w1[par][:, cols(f)]
                    if f == 0:
                        pe.wait_ge(e_xT_ready[0], n(0))
                    need(pe, e_ha_ready[(f + 2) % FB], n(0) if f >= 2 else n(-1))
                    mm(bank[2 + f % 2][:, :], w, e_xT[par][:, 0:GT]).then_inc(e_ha_psum[f], 1)
                    if f == 0:
                        pe.wait_ge(e_xT_ready[1], n(0))
                    need(pe, e_hb_ready[(f + 2) % FB], n(0) if f >= 2 else n(-1))
                    mm(bank[4 + f % 2][:, 0:CAP - GT], w, e_xT[par][:, GT:CAP]).then_inc(e_hb_psum[f], 1)
                if not final:
                    rows(e_x[1 - par], 1 - par, (((e + 1) >> 1) + 1) * 32)
                need(pe, e_y_ready[0], n(-1))
                for i in range(FULL + 1):
                    m = P if i < FULL else TAIL
                    dst = bank[6][:, cols(i)] if i < GC else bank[7][0:m, cols(i - GC)]
                    if i == GC:
                        need(pe, e_y_ready[1], n(-1))
                    for f in range(FB):
                        if i == 0:
                            pe.wait_ge(e_ha_ready[f], n(0))
                        if i == GC:
                            pe.wait_ge(e_hb_ready[f], n(0))
                        last = mm(dst, e_hT[:, f, P * i:P * i + m], e_w2[par][:, f, :], f == 0, f == FB - 1)
                    if i == GC - 1:
                        last.then_inc(e_y_psum[0], 1)
                last.then_inc(e_y_psum[1], 1)

            def experts():
                for s, k in ((probs_ready[GC - 1], FIRST), (qkv_read[GC - 1], FIRST + 1), (y_ready, FIRST),
                             (attn_added, FIRST - 1), (kT_ready, FIRST + 1), (q_ready, FIRST + 1)):
                    pe.wait_ge(s, k)
                run_experts(pe, expert)
                for s in (e_y_ready[1], e_ha_ready[FB - 1], e_hb_ready[FB - 1]):
                    pe.wait_ge(s, E)

            def free(name, t, n):
                got = before(name, t)
                if got is not None:
                    need(pe, got[0], n(got[1]))

            def project(t, n, j):
                need(pe, qkv_read[(j + 3) % GC], n(1) if j else n(0))
                if isinstance(t, int) and t == -1 and j == 0:
                    pe.wait_ge(v_centred, 1)
                mm(bank[2][:, 0:3 * P], xT[:, cols(j)], row(wqkv_all, layer_of(t + 1))).then_inc(qkv_psum[j], 1)

            halves = [slice(0, HP), slice(HP, P)]

            def scores(t, par, n, j):
                need_alone(pe, probs_ready[(j + 3) % GC], n(0) if j else n(-1))
                if j == 0:
                    if isinstance(t, int) and t == 0:
                        pe.wait_ge(g_slots, 1)
                    for s in (kT_ready, qa_ready, qb_ready):
                        need_alone(pe, s, n(0))
                for q in range(2):
                    for a in range(2):
                        c = slice(P * j + HP * a, P * j + HP * a + HP)
                        mm(bank[q][halves[a], 0:4 * HP], kT[halves[q], par, c], qT[halves[q], par, 0:4, c])
                for a in range(2):
                    last = mm(bank[a][:, 4 * HP:4 * HP + P], qk[halves[a], par, j, P:2 * P],
                              padded_heads(vpad[halves[a], par, j, :]))
                last.then_inc(scores_psum[j], 1)

            def values(par, n, j):
                if j == 0:
                    need(pe, y_ready, n(-1))
                pe.wait_ge(smask_ready[j], n(0))
                for a in range(2):
                    pe.matmul(bank[4 - a][:, cols(j, HP)], smask[:, (2 * j + a) % 4, :],
                              qT[:, par, 4, P * j + HP * a:P * j + HP * a + HP],
                              start=True, stop=False, skip_group_check=True)
                need_alone(pe, probs_ready[j], n(0))
                for h in range(H):
                    r = 32 * (h // 2)
                    for a in range(2):
                        last = pe.matmul(bank[4 - a][r:r + 32, cols(j, HP)], vpad[halves[a], par, j, cols(h, 32)],
                                         probs[halves[a], j % 2, h // 4, cols(h % 4, HP)], start=False,
                                         stop=h % 2 == 1, tile_position=(HP * a, r), skip_group_check=True)
                last.then_inc(av_done[j], 1)

            def transposes(name, src, done, width=P):
                for j in range(GC):
                    transpose(ring_bank(name)[:, cols(j, width)], src(j), done if j == GC - 1 else None)

            def step(t, par, n):
                s1, s2, s3, s4 = stages(t)
                if s1:
                    free("t1", t, n)
                    pe.wait_ge(xhat_ready, n(1))
                    transposes("t1", lambda j: xhat[:, j, :], t1_psum)
                if s2:
                    scores(t, par, n, 0)
                if s3:
                    free("var", t, n)
                    pe.wait_ge(y_ready, n(-1))
                    mm(ring_bank("var")[0:H, :], blockmean, ysq[:, :]).then_inc(var_psum, 1)
                if s1:
                    if isinstance(t, int) and t == -1:
                        pe.wait_ge(d_params, PARAMS)
                    pe.wait_ge(xT_ready, n(1))
                    project(t, n, 0)
                    free("g", t, n)
                    pe.wait_ge(wg_ready, n(1))
                    mm(ring_bank("g")[:, :], wg_now[:, :], xT[:, :]).then_inc(g_psum, 1)
                if s3:
                    free("vt", t, n)
                    need_alone(pe, var8_ready, n(-1))
                    transposes("vt", lambda j: var8[:, cols(j)], vt_psum, H)
                if s2:
                    scores(t, par, n, 1)
                    values(par, n, 0)
                if s1:
                    project(t, n, 1)
                if s4:
                    free("t2", t, n)
                    pe.wait_ge(x2hat_ready, n(-2))
                    transposes("t2", lambda j: xhat2[:, j, :], t2_psum)
                if s2:
                    scores(t, par, n, 2)
                    values(par, n, 1)
                if s4:
                    free("w1a", t, n)
                    pe.wait_ge(x2T_ready, n(-2))
                    pe.wait_ge(w1_ready, n(-2))
                    mm(ring_bank("w1a")[:, :], w1_now[:, 0:P], x2T[:, :]).then_inc(w1a_psum, 1)
                if s1:
                    project(t, n, 2)
                if s2:
                    scores(t, par, n, 3)
                if s4:
                    free("w1b", t, n)
                    mm(ring_bank("w1b")[:, :], w1_now[:, P:2 * P], x2T[:, :]).then_inc(w1b_psum, 1)
                if s1:
                    project(t, n, 3)
                if s2:
                    values(par, n, 2)
                if s3:
                    free("rt", t, n)
                    pe.wait_ge(rstdx_ready, n(-1))
                    transposes("rt", lambda j: rstdx[:, cols(j)], rt_psum)
                if s4:
                    free("w2", t, n)
                    pe.wait_ge(ha_ready, n(-2))
                    pe.wait_ge(hb_ready, n(-2))
                    wl = row(w2_all, layer_of(t - 2))
                    for j in range(GC):
                        for f in range(2):
                            last = mm(ring_bank("w2")[:, cols(j)], hT[:, f, cols(j)], wl[:, :, cols(f)], f == 0, f == 1)
                    last.then_inc(w2_psum, 1)
                if s1:
                    for j in range(GC):
                        pe.wait_ge(qk_ready[j], n(1))
                    free("tq", t, n)
                    transposes("tq", lambda j: qk[:, 1 - par, j, 0:P], tq_psum)
                    free("tk", t, n)
                    transposes("tk", lambda j: qk[:, 1 - par, j, P:2 * P], tk_psum)
                if s2:
                    values(par, n, 3)
                if s3:
                    free("wo", t, n)
                    pe.wait_ge(zT_ready, n(-1))
                    for j in range(GC):
                        last = mm(ring_bank("wo")[:, cols(j)], zT[:, cols(j)], row(wo_all, layer_of(t - 1)))
                    last.then_inc(wo_psum, 1)

            run_steps(pe, step, experts)

        @block.scalar
        def _(act):
            act.dma_start(gw_sb[:, :], gate).then_inc(d_gate, 16)
            for dst, src in ((wqkv_all, wqkv), (wg_all, wg), (ln_sb, ln), (b1_sb, eb1), (gn_sb, gn), (wo_all, wo),
                             (w1_all, w1), (w2_all, w2)):
                act.dma_start(dst[:], src).then_inc(d_params, 16)
            for k in range(2):
                rows = cols(k, SCH // 2)
                act.dma_start(ropec[:, rows, :], rope_c[:, rows, :]).then_inc(d_rope[k], 16)
                act.dma_start(ropes[:, rows, :], rope_s[:, rows, :]).then_inc(d_rope[k], 16)

            for g in range(NG + 1):
                if g < NG:
                    act.wait_ge(g_xT_psum, g + 1)
                    act.copy(xnT[g % 2], bank[g % 2][:, :]).then_inc(g_xT_ready, 1)
                if g >= 1:
                    act.wait_ge(g_lT_psum, g)
                    act.copy(lT[(g - 1) % 2], bank[2 + (g - 1) % 2][0:E, :]).then_inc(g_lT_ready, 1)
            act.wait_ge(g_shifted, 1)
            act.activation(gt["exp"], gt["shifted"], ACT.Exp).then_inc(g_exp, 1)

            def expert(e, par, n):
                for f in range(FB):
                    b = row(b1_sb, e * FB + f)
                    need_alone(act, e_ha_psum[f], n(0))
                    act.activation(e_hT[:, f, 0:GT], bank[2 + f % 2][:, :], ACT.Gelu, bias=b).then_inc(e_ha_ready[f], 1)
                    need_alone(act, e_hb_psum[f], n(0))
                    act.activation(e_hT[:, f, GT:CAP], bank[4 + f % 2][:, 0:CAP - GT], ACT.Gelu,
                                   bias=b).then_inc(e_hb_ready[f], 1)

            def next_first(k, n):
                if not isinstance(k, int) or k + 2 < STEPS:
                    act.wait_ge(t1_psum, n(2))
                    act.activation(xT[:, :], ring_bank("t1")[:, :], ACT.Identity, bias=ln_sb[:, 1:2],
                                   scale=ln_sb[:, 0:1]).then_inc(xT_ready, 1)
                if not isinstance(k, int) or 0 <= k < STEPS:
                    act.wait_ge(var_psum, n(0))
                    act.copy(var8[:, :], ring_bank("var")[0:H, :]).then_inc(var8_ready, 1)

            def experts():
                run_experts(act, expert)
                next_first(FIRST - 1, Counts(act, FIRST - 1))

            def as_row(ap):
                return ap.unsqueeze(1)

            act.wait_ge(d_params, PARAMS)
            act.copy(wg_now[:, :], wg_all[:, 0, :]).then_inc(wg_ready, 1)

            def step(t, par, n):
                s1, s2, s3, s4 = stages(t)
                if s1:
                    act.wait_ge(g_psum, n(1))
                    i = (t + 1) % 4 if isinstance(t, int) else (t + 1) & 3
                    act.activation(row(gateT, i), as_row(ring_bank("g")[:, :]), ACT.Silu).then_inc(gate_ready, 1)
                    if not isinstance(t, int) or t + 2 < STEPS:
                        act.copy(as_row(wg_now[:, :]), row(wg_all, layer_of(t + 2))).then_inc(wg_ready, 1)
                if s4:
                    act.wait_ge(t2_psum, n(-2))
                    act.activation(x2T[:, :], ring_bank("t2")[:, :], ACT.Identity, bias=ln_sb[:, 1:2],
                                   scale=ln_sb[:, 0:1]).then_inc(x2T_ready, 1)
                if s4:
                    act.wait_ge(w1a_psum, n(-2))
                    act.activation(hT[:, 0, :], ring_bank("w1a")[:, :], ACT.Gelu_apprx_tanh).then_inc(ha_ready, 1)
                if s3:
                    act.wait_ge(rstd_ready, n(-1))
                    act.copy(rstdx[:, :].rearrange("p (h d) -> p h d", d=DH),
                             rstd[:, :].unsqueeze(2).to_broadcast([P, GC * H, DH])).then_inc(rstdx_ready, 1)
                if s4:
                    act.wait_ge(w1b_psum, n(-2))
                    act.activation(hT[:, 1, :], ring_bank("w1b")[:, :], ACT.Gelu_apprx_tanh).then_inc(hb_ready, 1)
                if not isinstance(t, int) or 0 <= t - 1 < STEPS:
                    act.copy(as_row(w1_now[:, :]), row(w1_all, layer_of(t - 1))).then_inc(w1_ready, 1)
                if s1:
                    act.wait_ge(tq_psum, n(1))
                    act.copy(qT[:, 1 - par, 4, :], ring_bank("tq")[:, :]).then_inc(q_ready, 1)
                    act.wait_ge(tk_psum, n(1))
                    act.copy(kT[:, 1 - par, :], ring_bank("tk")[:, :]).then_inc(kT_ready, 1)
                    act.wait_ge(q_ready, n(1))
                    for v in range(2):
                        last = act.activation(qT[:, 1 - par, v, :], qT[:, 1 - par, 4, :], ACT.Copy,
                                              scale=cst[:, HEADMASK + v:HEADMASK + v + 1])
                    last.then_inc(qa_ready, 1)
                if s2:
                    act.wait_ge(av_done[GC - 1], n(0))
                    need(act, zT_ready, n(-1))
                    for a in range(2):
                        src = bank[4 - a][:, 0:GC * HP].rearrange("p (j n) -> p j n", j=GC)
                        dst = slice(a, 2 * GC, 2)
                        act.copy(ysb[:, :].rearrange("p (j n) -> p j n", n=HP)[:, dst, :], src)
                        last = act.activation(ysq[:, :].rearrange("p (j n) -> p j n", n=HP)[:, dst, :], src, ACT.Square)
                    last.then_inc(y_ready, 1)
                if not isinstance(t, int) or t + 1 != FIRST:
                    next_first(t, n)

            next_first(-2, Counts(act, -2))
            run_steps(act, step, experts)

        @block.vector
        def _(dve):
            links = [0]

            def link(ins):
                links[0] += 1
                ins.then_inc(chained, 1)
                dve.wait_ge(chained, links[0])

            def tt(out, a, b, op):
                return nc.vector.tensor_tensor(out, a, b, op)

            for k in range(4):
                dve.wait_ge(d_x[k], 16)
                for c in range(8):
                    last = nc.vector.bn_stats(stats[:, c, :], xin[:, 8 * k + c, :])
                link(last)
                for c in range(8):
                    last = nc.vector.bn_aggr(mv0[:, 8 * k + c, :], stats[:, c, :])
                link(last)
                nc.vector.tensor_scalar(ve0[:, cols(k, 8)], mv0[:, cols(k, 8), 1], EPS, None, ALU.add).then_inc(ln0_var, 1)
            for k in range(4):
                dve.wait_ge(ln0_rstd, k + 1)
                for c in range(8 * k, 8 * k + 8):
                    last = nc.vector.tensor_scalar(res[:, c, :], xin[:, c, :], mv0[:, c, 0:1], rs0[:, c:c + 1],
                                                   ALU.subtract, ALU.mult)
                last.then_inc(ln0_done, 1)

            def ln_apply(i, mv, rs, dst, done):
                x = group_rows(res, i)
                for j in range(GC):
                    last = nc.vector.tensor_scalar(dst[:, j, :], x[:, j, :], mv[:, j, 0:1], rs[:, j:j + 1],
                                                   ALU.subtract, ALU.mult)
                last.then_inc(done, 1)

            ln1 = (stats[:, 0:GC], mv1, ve1, ln1_st, ln1_mv, ln1_var)
            ln2 = (stats[:, GC:2 * GC], mv2, ve2, ln2_st, ln2_mv, ln2_var)

            def ln_stats(i, which, value):
                st, mv, ve, stat_done, mean_done, var_done = which
                x = group_rows(res, i)
                for j in range(GC):
                    last = nc.vector.bn_stats(st[:, j, :], x[:, j, :])
                last.then_inc(stat_done, 1)
                need_alone(dve, stat_done, value)
                for j in range(GC):
                    last = nc.vector.bn_aggr(mv[:, j, :], st[:, j, :])
                last.then_inc(mean_done, 1)
                dve.wait_ge(mean_done, value)
                nc.vector.tensor_scalar(ve[:, :], mv[:, :, 1], EPS, None, ALU.add).then_inc(var_done, 1)

            dve.wait_ge(ln0_done, 4)
            ln_stats(0, ln1, 1)
            dve.wait_ge(ln1_rstd, 1)
            ln_apply(0, mv1, rs1, xhat, xhat_ready)

            def by_chunk(ap):
                return ap.rearrange("p (c e) -> p c e", e=E)

            def by_expert(ap):
                return ap.rearrange("p (e c) -> p c e", e=E)

            def over_e(ap):
                return ap.unsqueeze(2).to_broadcast([P, NCH, E])

            revexp = cst[:, REVEXP:REVEXP + E].unsqueeze(1).to_broadcast([P, NCH, E])
            dve.wait_ge(g_logits, 1)
            link(nc.vector.tensor_copy(gt["logit"], bank[4][:, 0:256]))
            link(nc.vector.tensor_reduce(gsm["max"][:, :], by_chunk(gt["logit"]), AX.X, ALU.max))
            tt(by_chunk(gt["shifted"]), by_chunk(gt["logit"]), over_e(gsm["max"][:, :]), ALU.subtract).then_inc(g_shifted, 1)
            link(tt(by_chunk(gt["equal"]), by_chunk(gt["logit"]), over_e(gsm["max"][:, :]), ALU.is_equal))
            link(tt(by_chunk(gt["score"]), by_chunk(gt["equal"]), revexp, ALU.mult))
            link(nc.vector.tensor_reduce(gsm["rev"][:, :], by_chunk(gt["score"]), AX.X, ALU.max))
            tt(by_expert(gt["onehot"]), revexp, over_e(gsm["rev"][:, :]), ALU.is_equal).then_inc(g_onehot, 1)
            dve.wait_ge(g_exp, 1)
            link(nc.vector.tensor_reduce(gsm["sum"][:, :], by_chunk(gt["exp"]), AX.X, ALU.add))
            link(nc.vector.reciprocal(gsm["inv"][:, :], gsm["sum"][:, :]))
            dve.wait_ge(g_ranks, 1)
            link(nc.vector.tensor_tensor_scan(gt["scan"], cst[:, NOTFIRST:NOTFIRST + 256], bank[1][:, 0:256], 0.0,
                                              ALU.mult, ALU.add))
            link(tt(gt["scan"], gt["scan"], bank[1][:, 0:256], ALU.subtract))
            link(tt(gt["rank"], gt["scan"], bank[0][:, 0:256], ALU.add))
            link(tt(g_prod, gt["rank"], gt["onehot"], ALU.mult))
            link(nc.vector.tensor_reduce(gsm["rank"][:, :], by_expert(g_prod), AX.X, ALU.add))
            link(nc.vector.tensor_scalar(gsm["kept"][:, :], gsm["rank"][:, :], float(CAP), None, ALU.is_le))
            tt(weight[:, :], gsm["inv"][:, :], gsm["kept"][:, :], ALU.mult)
            nc.vector.tensor_scalar(gsm["far"][:, :], gsm["kept"][:, :], -1e6, 1e6, ALU.mult, ALU.add)
            link(nc.vector.scalar_tensor_tensor(out=gsm["slot"][:, :], in0=gsm["rev"][:, :], scalar=-float(CAP),
                                                in1=gsm["rank"][:, :], op0=ALU.mult, op1=ALU.add))
            nc.vector.scalar_tensor_tensor(out=slots[:, :], in0=gsm["slot"][:, :], scalar=float(E * CAP - 1),
                                           in1=gsm["far"][:, :], op0=ALU.add, op1=ALU.add).then_inc(g_slots, 1)

            dve.wait_ge(d_params, PARAMS)
            wv = wqkv_all[:, :, 2 * P:3 * P].rearrange("p l (h d) -> p l h d", d=DH)
            mean = vare[:, :].rearrange("p (l h) -> p l h", l=L)
            link(nc.vector.tensor_reduce(mean, wv, AX.X, ALU.add))
            link(nc.vector.tensor_scalar(mean, mean, -1.0 / DH, None, ALU.mult))
            for l in range(L):
                last = tt(wv[:, l], wv[:, l], mean[:, l, :].unsqueeze(2).to_broadcast([P, H, DH]), ALU.add)
            last.then_inc(v_centred, 1)
            nc.vector.memset(flat(state), 0.0).then_inc(prepared, 1)
            dve.wait_ge(prepared, 1)

            def expert(e, par, n):
                half = (e >> 1) if not isinstance(e, int) else e // 2
                def take(parity, k):
                    dve.wait_ge(e_rows_psum[0], k)
                    nc.vector.tensor_copy(e_xT[parity][:, 0:GT], bank[0][:, :]).then_inc(e_xT_ready[0], 1)
                    dve.wait_ge(e_rows_psum[1], k)
                    nc.vector.tensor_copy(e_xT[parity][:, GT:CAP], bank[1][:, 0:CAP - GT]).then_inc(e_xT_ready[1], 1)

                if isinstance(e, int) and e == 0:
                    take(0, 1)
                if not (isinstance(e, int) and e == E - 1):
                    take(1 - par, n(1))
                dve.wait_ge(d_ew[par], (half + 1) * 48)
                dve.wait_ge(d_ey[par], half * 32) if not isinstance(half, int) or half > 0 else None
                dve.wait_ge(e_y_psum[0], n(0))
                tt(e_y[par][:, 0:GC, :], bank[6][:, :].rearrange("p (i d) -> p i d", d=D),
                   e_b2[par].unsqueeze(1).to_broadcast([P, GC, D]), ALU.add).then_inc(e_y_ready[0], 1)
                dve.wait_ge(e_y_psum[1], n(0))
                tt(e_y[par][:, GC, :], bank[7][:, 0:P], e_b2[par], ALU.add)
                tt(e_y[par][0:1, FULL, :], bank[7][0:1, P:2 * P], e_b2[par][0:1, :], ALU.add).then_inc(e_y_ready[1], 1)

            def experts():
                run_experts(dve, expert)

            def scores(t, n, j):
                need(dve, state_ready[(j + 3) % GC], n(0) if j else n(-1))
                need(dve, smask_ready[(j + 3) % GC], n(0) if j else n(-1))
                need(dve, av_done[(j + 2) % GC], n(0) if j >= 2 else n(-1))
                g = group_of(t) & (GC - 1)
                keep, deckeep = (row(cst, g + KEEP), row(cst, g + DECKEEP)) if j == 0 else (1.0, cst[:, DECAY:DECAY + 1])

                def masked(a, keep):
                    return nc.vector.scalar_tensor_tensor(out=smask[:, (2 * j + a) % 4, :], in0=state[:, a, :], scalar=keep,
                                                          in1=blockdec, op0=ALU.mult, op1=ALU.mult)

                def with_half(a, decay):
                    return nc.vector.scalar_tensor_tensor(out=state[:, 1 - a, :], in0=state[:, a, :], scalar=decay,
                                                          in1=bank[a][:, 4 * HP:4 * HP + P], op0=ALU.mult, op1=ALU.add)

                def causal_scores(q):
                    return tt(probs[:, j % 2, q, :].rearrange("p (v n) -> p v n", v=4),
                              bank[q][:, 0:4 * HP].rearrange("p (v n) -> p v n", v=4),
                              causal.unsqueeze(1).to_broadcast([P, 4, HP]), ALU.mult)

                masked(0, keep)
                dve.wait_ge(scores_psum[j], n(0))
                with_half(0, deckeep).then_inc(half_ready[j], 1)
                causal_scores(0)
                dve.wait_ge(half_ready[j], n(0))
                with_half(1, cst[:, DECAY:DECAY + 1]).then_inc(state_ready[j], 1)
                causal_scores(1).then_inc(probs_ready[j], 1)
                masked(1, 1.0).then_inc(smask_ready[j], 1)

            def rotate(t, par, n, j):
                if isinstance(t, int) and t in (-1, 1) and j == 0:
                    dve.wait_ge(d_rope[(t + 1) // 2], 32)
                if isinstance(t, int) and t == -1 and j == 0:
                    dve.wait_ge(cleared, 2)
                dve.wait_ge(qkv_psum[j], n(1))
                nc.vector.tensor_copy(padded_heads(vpad[:, 1 - par, j, :]),
                                      bank[2][:, 2 * P:3 * P].rearrange("p (r w d) -> p r w d", r=4, w=2))
                need(dve, qk_ready[(j + 2) % GC], n(1) if j >= 2 else n(0))
                src = bank[2][:, 0:2 * P].unsqueeze(1)
                tt(rc[:, j % 2:j % 2 + 1, :], src, chunk_row(ropec, t + 1, j), ALU.mult)

                def pairs(ap):
                    return ap.rearrange("p a (h s d) -> p (a h) s d", s=2, d=DH // 2)

                tt(pairs(rs_[:, j % 2:j % 2 + 1, :]), pairs(src)[:, :, ::-1, :],
                   pairs(chunk_row(ropes, t + 1, j)), ALU.mult).then_inc(qkv_read[j], 1)

            def output(g):
                x = xin[:, cols(g, GC), :]
                tt(x, x, res[:, cols(g, GC), :], ALU.add).then_inc(summed, 1)
                dve.wait_ge(summed, g + 1)
                for c in range(GC * g, GC * g + GC):
                    last = nc.vector.scalar_tensor_tensor(out=xin[:, c, :], in0=routed[:, c, :],
                                                          scalar=weight[:, c:c + 1], in1=xin[:, c, :],
                                                          op0=ALU.mult, op1=ALU.add)
                last.then_inc(out_ready, 1)

            def step(t, par, n):
                s1, s2, s3, s4 = stages(t)
                s0 = not isinstance(t, int) or t + 2 < STEPS
                if s2:
                    scores(t, n, 0)
                if s1:
                    rotate(t, par, n, 0)
                if s3:
                    dve.wait_ge(vt_psum, n(-1))
                    nc.vector.tensor_scalar(vare[:, :], ring_bank("vt")[:, 0:GC * H], EPS, None,
                                            ALU.add).then_inc(vare_ready, 1)
                if s4:
                    dve.wait_ge(ln2_rstd, n(-2))
                    ln_apply(t - 2, mv2, rs2, xhat2, x2hat_ready)
                if s2:
                    scores(t, n, 1)
                if s1:
                    rotate(t, par, n, 1)
                if s0:
                    ln_stats(t + 2, ln1, n(2))
                if s2:
                    scores(t, n, 2)
                if s1:
                    rotate(t, par, n, 2)
                if s0:
                    dve.wait_ge(ln1_rstd, n(2))
                    need(dve, t1_psum, n(1))
                    ln_apply(t + 2, mv1, rs1, xhat, xhat_ready)
                if s2:
                    scores(t, n, 3)
                if s1:
                    rotate(t, par, n, 3)
                if s3:
                    dve.wait_ge(rt_psum, n(-1))
                    l = layer_of(t - 1)
                    nc.vector.scalar_tensor_tensor(out=ysb[:, :], in0=ring_bank("rt")[:, :], scalar=row(gn_sb, l),
                                                   in1=ysb[:, :], op0=ALU.mult, op1=ALU.mult).then_inc(z1_ready, 1)
                    dve.wait_ge(z1_ready, n(-1))
                    i = (t - 1) % 4 if isinstance(t, int) else (t - 1) & 3
                    nc.vector.scalar_tensor_tensor(out=zT[:, :].unsqueeze(1), in0=ysb[:, :].unsqueeze(1),
                                                   scalar=row(gn_sb, l + L), in1=row(gateT, i), op0=ALU.add,
                                                   op1=ALU.mult).then_inc(zT_ready, 1)
                if s4:
                    dve.wait_ge(w2_psum, n(-2))
                    x = group_rows(res, t - 2)
                    tt(x, x, ring_bank("w2")[:, :].rearrange("p (j d) -> p j d", d=D), ALU.add).then_inc(ffn_added, 1)
                if s1:
                    dve.wait_ge(q_ready, n(1))
                    for v in range(2, 4):
                        last = nc.vector.tensor_scalar(qT[:, 1 - par, v, :], qT[:, 1 - par, 4, :],
                                                       cst[:, HEADMASK + v:HEADMASK + v + 1], None, ALU.mult)
                    last.then_inc(qb_ready, 1)
                if s3:
                    if isinstance(t, int) and t == 1:
                        dve.wait_ge(d_scatter[0], 16 * GC * len(FIRST_GROUPS[0]))
                    dve.wait_ge(wo_psum, n(-1))
                    x = group_rows(res, t - 1)
                    tt(x, x, ring_bank("wo")[:, :].rearrange("p (j d) -> p j d", d=D), ALU.add).then_inc(attn_added, 1)
                    need_alone(dve, attn_added, n(-1))
                    ln_stats(t - 1, ln2, n(-1))
                if isinstance(t, int) and t >= STEPS - 1:
                    if t == STEPS + 1:
                        dve.wait_ge(ffn_added, STEPS)
                    groups = LAST_GROUPS[t - (STEPS - 1)]
                    dve.wait_ge(d_gather[t - (STEPS - 1)], 16 * GC * len(groups))
                    for g in groups:
                        output(g)

            run_steps(dve, step, experts)

        @block.gpsimd
        def _(pool):
            nc.gpsimd.memset(zeros, 0.0).then_inc(zeroed, 1)
            nc.gpsimd.memset(power[:, :], -0.5).then_inc(cleared, 1)
            nc.gpsimd.memset(vpad[:].rearrange("p a b c -> p (a b c)"), 0.0).then_inc(cleared, 1)
            pool.wait_ge(cleared, 2)

            def reciprocal_root(out, v):
                return nc.gpsimd.tensor_tensor(out, v, power[:, 0:v.shape[1]], ALU.pow)

            for k in range(4):
                pool.wait_ge(ln0_var, k + 1)
                reciprocal_root(rs0[:, cols(k, 8)], ve0[:, cols(k, 8)]).then_inc(ln0_rstd, 1)

            pool.wait_ge(ln1_var, 1)
            reciprocal_root(rs1[:, :], ve1[:, :]).then_inc(ln1_rstd, 1)

            def scatter(g, done):
                for c in range(GC * g, GC * g + GC):
                    nc.gpsimd.indirect_dma_start(
                        out=slot_x, out_offset=bass.IndirectOffsetOnAxis(ap=slots[:, c:c + 1], axis=0),
                        in_=res[:, c, :], in_offset=None, bounds_check=E * CAP - 1,
                        oob_is_err=False).then_inc(done, 16)

            def gather(g, done):
                for c in range(GC * g, GC * g + GC):
                    nc.gpsimd.indirect_dma_start(
                        out=routed[:, c, :], out_offset=None, in_=slot_y,
                        in_offset=bass.IndirectOffsetOnAxis(ap=slots[:, c:c + 1], axis=0),
                        bounds_check=E * CAP - 1, oob_is_err=False).then_inc(done, 16)

            slot_tiles = slot_y.rearrange("(e r) d -> e r d", e=E)

            def expert(e, par, n):
                dst = slot_tiles[e:e + 1] if isinstance(e, int) else slot_tiles[bass.ds(e, 1)]
                pool.wait_ge(e_y_ready[1], n(0))
                pool.dma_start(dst[:, 0:FULL * P, :].rearrange("a (i p) d -> p (a i) d", p=P),
                               e_y[par][:, 0:FULL, :]).then_inc(d_ey[par], 16)
                pool.dma_start(dst[:, FULL * P:CAP, :].rearrange("a r d -> (a r) d"),
                               e_y[par][0:1, FULL, :]).then_inc(d_ey[par], 16)

            def experts():
                run_experts(pool, expert)

            def rotated(par, n, j):
                pool.wait_ge(qkv_read[j], n(1))
                nc.gpsimd.tensor_tensor(qk[:, 1 - par, j, :], rc[:, j % 2, :], rs_[:, j % 2, :], ALU.add).then_inc(qk_ready[j], 1)

            def step(t, par, n):
                s1, s2, s3, s4 = stages(t)
                if s1:
                    rotated(par, n, 0)
                if s3:
                    pool.wait_ge(vare_ready, n(-1))
                    reciprocal_root(rstd[:, :], vare[:, :]).then_inc(rstd_ready, 1)
                mine = FIRST_GROUPS[t + 1] if isinstance(t, int) and t + 1 < len(FIRST_GROUPS) else ()
                if mine:
                    if t == -1:
                        pool.wait_ge(g_slots, 1)
                        pool.wait_ge(ln0_done, 4)
                        pool.wait_ge(d_zero, 16 * (E * D // P))
                    for g in mine[:-1]:
                        scatter(g, d_scatter[t + 1])
                if s1:
                    rotated(par, n, 1)
                if not isinstance(t, int) or t + 2 < STEPS:
                    pool.wait_ge(ln1_var, n(2))
                    reciprocal_root(rs1[:, :], ve1[:, :]).then_inc(ln1_rstd, 1)
                if s1:
                    rotated(par, n, 2)
                if mine:
                    scatter(mine[-1], d_scatter[t + 1])
                if s1:
                    rotated(par, n, 3)
                if s3:
                    pool.wait_ge(ln2_var, n(-1))
                    reciprocal_root(rs2[:, :], ve2[:, :]).then_inc(ln2_rstd, 1)
                if isinstance(t, int) and STEPS - 2 <= t <= STEPS:
                    if t == STEPS - 2:
                        for k in range(2):
                            pool.wait_ge(d_ey[k], 32 * (E // 2))
                        nc.gpsimd.memset(flat(routed), 0.0).then_inc(cleared, 1)
                        pool.wait_ge(cleared, 3)
                    for g in LAST_GROUPS[t - (STEPS - 2)]:
                        gather(g, d_gather[t - (STEPS - 2)])

            run_steps(pool, step, experts)


def kernel(**inputs):
    import concourse.bacc as _bacc
    from concourse.bass_utils import run_bass_kernel_spmd as _run

    a = {k: np.asarray(v) for k, v in inputs.items()}
    B, S, D = a["L0_attn_X"].shape
    H, DH = 8, 16
    order = np.arange(D).reshape(H, DH // 2, 2).transpose(0, 2, 1).reshape(D)
    qkv = [a["L0_attn_Wq"][:, :, order], a["L0_attn_Wk"][:, :, order], a["L0_attn_Wv"]]
    L, F = a["L0_attn_W1"].shape[0], a["L0_attn_W1"].shape[2]
    consts, rope_c, rope_s = shape_constants(S, H, DH)
    arrays = {
        "x": a["L0_attn_X"].reshape(B * S, D),
        "wqkv": np.concatenate(qkv, axis=2).transpose(1, 0, 2),
        "wg": a["L0_attn_Wg"].transpose(1, 0, 2),
        "wo": a["L0_attn_Wo"].transpose(1, 0, 2),
        "w1": a["L0_attn_W1"].transpose(1, 0, 2),
        "w2": a["L0_attn_W2"].reshape(L, F // P, P, D).transpose(2, 0, 1, 3).reshape(P, L, (F // P) * D),
        "ln": np.stack([a["L0_attn_ln_scale"], a["L0_attn_ln_bias"]], axis=1),
        "gn": np.concatenate([a["L0_attn_gn_scale"], a["L0_attn_gn_bias"]], axis=0).T,
        "gate": a["L0_ffn_wg"],
        "ew1": a["L0_ffn_W1"],
        "eb1": a["L0_ffn_b1"].reshape(a["L0_ffn_b1"].shape[0], -1, P).transpose(2, 0, 1).reshape(P, -1),
        "ew2": a["L0_ffn_W2"],
        "eb2": a["L0_ffn_b2"],
        "consts": consts,
        "rope_c": rope_c,
        "rope_s": rope_s,
    }
    arrays = {f"in_{k}": np.ascontiguousarray(v) for k, v in arrays.items()}
    nc = _bacc.Bacc("TRN2", target_bir_lowering=False, num_devices=1)
    args = [nc.dram_tensor(k, v.shape, mybir.dt.from_np(v.dtype), kind="ExternalInput").ap() for k, v in arrays.items()]
    args.append(nc.dram_tensor("out_0", (B * S, D), F32, kind="ExternalOutput").ap())
    retention_moe(nc, *args)
    r = _run(nc, [arrays], core_ids=[0])
    return r.results[0]["out_0"].reshape(B, S, D)
```

```python
from contextlib import ExitStack

import numpy as np

import concourse.bass as bass
from concourse import mybir
from concourse.alu_op_type import AluOpType as ALU

F32 = mybir.dt.float32
I32 = mybir.dt.int32
U32 = mybir.dt.uint32
ACT = mybir.ActivationFunctionType
AX = mybir.AxisListType

P = 128
GC = 4
GT = GC * P
HP = P // 2
EPS = 1e-5

IDENT = 0
TRI = IDENT + P
CAUSAL = TRI + P
ONES = CAUSAL + HP
BLOCKDEC = ONES + P
HEADMASK = BLOCKDEC + P
BLOCKMEAN = HEADMASK + 4
DECAY = BLOCKMEAN + 8
KEEP = DECAY + 1
DECKEEP = KEEP + 4
REVEXP = DECKEEP + 4
NOTFIRST = REVEXP + 8
CONSTS = NOTFIRST + 8 * 32


def shape_constants(S, H, DH):
    D = H * DH
    half = DH // 2
    f32 = np.float32
    ends = np.log(1 / 32), np.log(1 / 64)
    gam = (1.0 - np.exp(np.linspace(ends[0], ends[1], H).astype(f32))).astype(f32)
    lg = np.log(gam).astype(f32).astype(np.float64)
    inv = (f32(1.0) / np.power(f32(10000.0), np.arange(0, DH, 2, dtype=f32) / f32(DH))).astype(f32)
    ang = (np.arange(S, dtype=f32)[:, None] * inv[None, :]).astype(f32).astype(np.float64)
    cos, sin = np.cos(ang), np.sin(ang)
    within = np.arange(S) % HP
    qd = np.exp(within[:, None] * lg)
    kd = np.exp(-within[:, None] * lg)

    def table(first, second, decay):
        t = np.concatenate([first, second], axis=1)[:, None, :] * decay[:, :, None]
        return t.reshape(S, D)

    rope_c = np.concatenate([table(cos, cos, qd), table(cos, cos, kd)], axis=1)
    rope_s = np.concatenate([table(-sin, sin, qd), table(sin, -sin, kd)], axis=1)
    rope_c, rope_s = (
        np.ascontiguousarray(t.reshape(S // P, P, 2 * D).transpose(1, 0, 2)).astype(f32)
        for t in (rope_c, rope_s)
    )
    c = np.zeros((P, CONSTS), f32)
    feat = np.arange(P) // DH
    dec = np.exp(HP * lg)[feat]
    c[:, IDENT:IDENT + P] = np.eye(P)
    c[:, TRI:TRI + P] = np.triu(np.ones((P, P))) - 1
    c[:, CAUSAL:CAUSAL + HP] = np.tile(np.triu(np.ones((HP, HP))), (2, 1))
    c[:, ONES:ONES + P] = 1.0
    c[:, BLOCKDEC:BLOCKDEC + P] = (feat[:, None] == feat[None, :]) * dec[:, None]
    for v in range(4):
        c[:, HEADMASK + v] = feat % 4 == v
    for h in range(H):
        c[:, BLOCKMEAN + h] = (feat == h) / DH
    c[:, DECAY] = dec
    for g in range(4):
        c[:, KEEP + g] = g > 0
        c[:, DECKEEP + g] = dec * (g > 0)
    c[:, REVEXP:REVEXP + 8] = 8 - np.arange(8)
    c[:, NOTFIRST:] = np.tile(np.arange(32) > 0, 8)
    return c, rope_c, rope_s


def retention_moe(nc, x, wqkv, wg, wo, w1, w2, ln, gn, gate, ew1, eb1, ew2, eb2,
                  consts, rope_c, rope_s, out):
    NTOK, D = x.shape
    NCH = NTOK // P
    NG = NCH // GC
    SCH = rope_c.shape[1]
    L = wo.shape[1]
    H, DH = 8, 16
    E, _, FE = ew1.shape
    FB = FE // P
    CAP = int(NTOK / E * 1.25) + 1
    FULL = CAP // P
    TAIL = CAP - FULL * P
    assert D == P and TAIL == 1 and FULL == 5 and NG == 8 and L == 4
    STEPS = L * NG
    EXPERTS_AT = 1
    FIRST, LAST = 2, STEPS - 3
    UNROLL = 4
    assert (LAST - FIRST + 1) % UNROLL == 0
    PARAMS = 16 * 8
    SCATTERS = [[range(0, 0), range(0, 5), range(5, 8), range(8, 19)],
                [range(19, 21), range(21, 26), range(26, 29), range(29, NCH)]]

    with ExitStack() as ctx:
        def sb(name, shape, dt=F32):
            return ctx.enter_context(nc.sbuf_tensor(name, shape, dt))

        def sem(name):
            return ctx.enter_context(nc.semaphore(name))

        def sems(name, n):
            return [sem(f"{name}{i}") for i in range(n)]

        bank = [ctx.enter_context(nc.psum_tensor(f"bank{i}", [P, 512], F32)) for i in range(8)]

        cst = sb("cst", [P, CONSTS])
        ident, tri, ones = (cst[:, o:o + P] for o in (IDENT, TRI, ONES))
        causal = cst[:, CAUSAL:CAUSAL + HP]
        blockdec = cst[:, BLOCKDEC:BLOCKDEC + P]
        blockmean = cst[:, BLOCKMEAN:BLOCKMEAN + H]
        xin = sb("xin", [P, NCH, D])
        res = sb("res", [P, NCH, D])
        ropec = sb("ropec", [P, SCH, 2 * D])
        ropes = sb("ropes", [P, SCH, 2 * D])
        wqkv_all = sb("wqkv_all", [P, L, 3 * D])
        wg_all = sb("wg_all", [P, L, D])
        wo_all = sb("wo_all", [P, L, D])
        w1_all = sb("w1_all", [P, L, 2 * D])
        w2_all = sb("w2_all", [P, L, 2 * D])
        ln_sb = sb("ln_sb", [P, 2])
        gn_sb = sb("gn_sb", [P, 2 * L])
        power = sb("power", [P, 32])
        stats = sb("stats", [P, 8, 6])
        weight = sb("weight", [P, NCH])
        slots = sb("slots", [P, NCH], U32)

        slot_now = sb("slot_now", [P, 1], U32)
        rows_now = sb("rows_now", [P, 1, D])

        xhat = sb("xhat", [P, GC, D])
        xT = sb("xT", [P, GT])
        xhat2 = sb("xhat2", [P, GC, D])
        x2T = sb("x2T", [P, GT])
        wg_now = sb("wg_now", [P, D])
        w1_now = sb("w1_now", [P, 2 * D])
        gateT = sb("gateT", [P, 4, GT])
        rc = sb("rc", [P, 2, 2 * D])
        rs_ = sb("rs_", [P, 2, 2 * D])
        qk = sb("qk", [P, 2, GC, 2 * D])
        vpad = sb("vpad", [P, 2, GC, 2 * D])
        qT = sb("qT", [P, 2, 5, GT])
        kT = sb("kT", [P, 2, GT])
        probs = sb("probs", [P, 2, 2, 4 * HP])
        state = sb("state", [P, 2, HP])
        smask = sb("smask", [P, 4, D])
        ysb = sb("ysb", [P, GT])
        ysq = sb("ysq", [P, GT])
        vare = sb("vare", [P, GC * H])
        rstd = sb("rstd", [P, GC * H])
        rstdx = sb("rstdx", [P, GT])
        zT = sb("zT", [P, GT])
        hT = sb("hT", [P, 2, GT])
        mv1 = sb("mv1", [P, GC, 2])
        ve1 = sb("ve1", [P, GC])
        rs1 = sb("rs1", [P, GC])
        mv2 = sb("mv2", [P, GC, 2])
        ve2 = sb("ve2", [P, GC])
        rs2 = sb("rs2", [P, GC])

        gw_sb = sb("gw_sb", [P, E])
        b1_sb = sb("b1_sb", [P, E * FB])
        mv0 = sb("mv0", [P, NCH, 2])
        ve0 = sb("ve0", [P, NCH])
        rs0 = sb("rs0", [P, NCH])
        gsm = {n: sb("g_" + n, [P, NCH]) for n in ("max", "sum", "inv", "rev", "rank", "kept", "slot", "far")}
        e_hT = sb("e_hT", [P, FB, CAP])
        zeros = e_hT[:, 0, :]
        e_room = sb("e_room", [P, 26 * 256 + 2])

        def room(at, *shape):
            n = int(np.prod(shape))
            ap = e_room[:, at * 256:at * 256 + n]
            return ap if len(shape) == 1 else ap.rearrange("p (a b) -> p a b", b=shape[1])

        e_w1 = [room(2 * k, GT) for k in range(2)]
        e_w2 = [room(4 + 2 * k, FB, D) for k in range(2)]
        e_x = [room(8 + 3 * k, FULL + 1, D) for k in range(2)]
        e_y = [room(14 + 3 * k, FULL + 1, D) for k in range(2)]
        e_b2 = [e_room[:, 20 * 256 + D * k:20 * 256 + D * (k + 1)] for k in range(2)]
        e_xT = [e_room[:, 21 * 256 + CAP * k:21 * 256 + CAP * (k + 1)] for k in range(2)]
        routed = room(0, NCH - (LAST + 1 - FIRST), D)
        gt = {n: room(8 + i, 256) for i, n in enumerate(
            ("shifted", "exp", "equal", "score", "onehot", "scan", "rank"))}
        g_prod = room(16, 256)
        xnT = [room(17 + 2 * k, GT) for k in range(2)]
        lT = [room(21 + 2 * k, GT)[0:E, :] for k in range(2)]

        slot_x = nc.dram_tensor("slot_x", [E * CAP, D], F32, kind="Internal").ap()
        slot_y = nc.dram_tensor("slot_y", [E * CAP, D], F32, kind="Internal").ap()
        x_dram = x.rearrange("(c p) d -> p c d", p=P)
        out_dram = out.rearrange("(c p) d -> p c d", p=P)

        d_const, d_gate, d_params, d_zero = (sem(n) for n in ("d_const", "d_gate", "d_params", "d_zero"))
        d_rope = sems("d_rope", 2)
        d_scatter, d_gather, d_gather_last = sems("d_scatter", len(SCATTERS)), sem("d_gather"), sem("d_gather_last")
        d_x = sems("d_x", 4)
        d_ew, d_ex, d_ey = sems("d_ew", 2), sems("d_ex", 2), sems("d_ey", 2)
        d_out = sem("d_out")
        def named(names):
            return (sem(name) for name in names.split())

        zeroed, cleared, v_centred, state_zero, ln0_var, ln0_rstd, ln0_done = named(
            "zeroed cleared v_centred state_zero ln0_var ln0_rstd ln0_done")
        g_xT_psum, g_xT_ready, g_lT_psum, g_lT_ready, g_logits = named(
            "g_xT_psum g_xT_ready g_lT_psum g_lT_ready g_logits")
        g_shifted, g_exp, g_onehot, g_ranks, g_slots, chained = named(
            "g_shifted g_exp g_onehot g_ranks g_slots chained")
        e_rows_psum, e_xT_ready, e_y_psum, e_y_ready = (
            sems(n, 2) for n in ("e_rows_psum", "e_xT_ready", "e_y_psum", "e_y_ready"))
        e_ha_psum, e_hb_psum, e_ha_ready, e_hb_ready = (
            sems(n, FB) for n in ("e_ha_psum", "e_hb_psum", "e_ha_ready", "e_hb_ready"))
        t1_psum, t2_psum, var_psum, g_psum, w1a_psum, w1b_psum = named(
            "t1_psum t2_psum var_psum g_psum w1a_psum w1b_psum")
        rt_psum, w2_psum, wo_psum, tq_psum, tk_psum = named("rt_psum w2_psum wo_psum tq_psum tk_psum")
        ln1_st, ln1_mv, ln1_var, ln1_rstd, xhat_ready, xT_ready = named(
            "ln1_st ln1_mv ln1_var ln1_rstd xhat_ready xT_ready")
        ln2_st, ln2_mv, ln2_var, ln2_rstd, x2hat_ready, x2T_ready = named(
            "ln2_st ln2_mv ln2_var ln2_rstd x2hat_ready x2T_ready")
        q_ready, qa_ready, qb_ready, kT_ready, gate_ready, wg_ready, w1_ready = named(
            "q_ready qa_ready qb_ready kT_ready gate_ready wg_ready w1_ready")
        y_ready, vare_ready, rstd_ready, rstdx_ready, z1_ready, zT_ready, attn_added = named(
            "y_ready vare_ready rstd_ready rstdx_ready z1_ready zT_ready attn_added")
        ha_ready, hb_ready, ffn_added = named("ha_ready hb_ready ffn_added")
        scores_psum, probs_ready, av_done, qkv_psum, smask_ready, half_ready, state_ready, qkv_read, qk_ready = (
            sems(n, GC) for n in ("scores_psum", "probs_ready", "av_done", "qkv_psum", "smask_ready",
                                  "half_ready", "state_ready", "qkv_read", "qk_ready"))
        merged, summed, out_ready, slot_ready = named("merged summed out_ready slot_ready")
        passed = {e: sem(f"passed_{e.value}") for e in (
            nc.tensor.engine, nc.scalar.engine, nc.vector.engine, nc.gpsimd.engine)}

        USES = [
            ("t1", 1, xT_ready), ("wo", -2, attn_added), ("var", -1, vare_ready), ("g", 1, gate_ready),
            ("t2", -2, x2T_ready), ("w1a", -2, ha_ready), ("w1b", -2, hb_ready), ("rt", -1, z1_ready),
            ("w2", -2, ffn_added), ("tq", 1, q_ready), ("tk", 1, kT_ready), ("none", 0, None),
        ]
        PLACE = {name: i for i, (name, _, _) in enumerate(USES)}

        def ring_bank(name):
            return bank[5 + PLACE[name] % 3]

        def before(name, t):
            k = PLACE[name] - 3
            while True:
                who, off, s = USES[k % len(USES)]
                off += k // len(USES)
                if not isinstance(t, int) and s is not None:
                    return s, off
                if isinstance(t, int) and k // len(USES) + t < -1:
                    return None
                if isinstance(t, int) and s is not None and 0 <= t + off < STEPS:
                    return s, off
                k -= 3

        class Counts:

            def __init__(self, eng, t):
                self.t, self.fixed = t, isinstance(t, int)
                self.reg = None if self.fixed else {k: eng.snap(t + (k + 1)) for k in range(-2, 3)}

            def __call__(self, k):
                return self.t + k + 1 if self.fixed else self.reg[k]

        def need(eng, s, value):
            if not isinstance(value, int) or value > 0:
                eng.wait_ge(s, value)

        def need_alone(eng, s, value):
            need(eng, s, value)
            if not isinstance(value, int):
                eng.sem_inc(passed[eng.engine], 1)

        def stages(t):
            if not isinstance(t, int):
                return True, True, True, True
            return tuple(0 <= t + k < STEPS for k in (1, 0, -1, -2))

        def run_steps(eng, step, experts):
            for t in range(-1, FIRST):
                if t == EXPERTS_AT:
                    experts()
                step(t, t % 2, Counts(eng, t))
            with eng.Fori(0, (LAST - FIRST + 1) // UNROLL) as i:
                for k in range(UNROLL):
                    t = i * UNROLL + (FIRST + k)
                    step(t, (FIRST + k) % 2, Counts(eng, t))
            for t in range(LAST + 1, STEPS + 2):
                step(t, t % 2, Counts(eng, t))

        def run_experts(eng, expert):
            for e in (0, 1):
                expert(e, e, Counts(eng, e))
            with eng.Fori(0, (E - 4) // 2) as i:
                for k in range(2):
                    e = i * 2 + (2 + k)
                    expert(e, k, Counts(eng, e))
            for e in (E - 2, E - 1):
                expert(e, e % 2, Counts(eng, e))

        def layer_of(i):
            return (i // NG) if isinstance(i, int) else (i >> 3) & (L - 1)

        def group_of(i):
            return i % NG if isinstance(i, int) else i & (NG - 1)

        def row(ap, i):
            return ap[:, i:i + 1] if isinstance(i, int) else ap[:, bass.ds(i, 1)]

        def group_rows(ap, i):
            g = group_of(i)
            if isinstance(g, int):
                return ap[:, GC * g:GC * g + GC, :]
            return ap[:, bass.ds(g * GC, GC), :]

        def chunk_row(ap, i, j):
            c = (group_of(i) & (ap.shape[1] // GC - 1)) * GC + j
            return row(ap, c)

        def cols(j, n=P):
            return slice(n * j, n * j + n)

        def flat(ap):
            return ap.rearrange("p a b -> p (a b)")

        def padded_heads(ap):
            return ap.rearrange("p (r w d) -> p r w d", w=4, d=DH)[:, :, 0:4:3, :]

        block = ctx.enter_context(nc.Block())

        @block.sync
        def _(sp):
            for k in range(4):
                sp.dma_start(xin[:, cols(k, 8), :], x_dram[:, cols(k, 8), :]).then_inc(d_x[k], 16)
                if k == 1:
                    sp.dma_start(cst[:], consts).then_inc(d_const, 16)
            sp.wait_ge(zeroed, 1)
            slot_rows = slot_x.rearrange("r d -> (r d)").rearrange("(p k) -> p k", p=P)
            for k in range(E * CAP * D // P // CAP):
                sp.dma_start(slot_rows[:, cols(k, CAP)], zeros[:, :]).then_inc(d_zero, 16)

            def load_weights(e, par):
                a = ew1[bass.ds(e, 1)] if not isinstance(e, int) else ew1[e:e + 1]
                b = ew2[bass.ds(e, 1)] if not isinstance(e, int) else ew2[e:e + 1]
                sp.dma_start(e_w1[par], a.rearrange("a p f -> (a p) f")).then_inc(d_ew[par], 16)
                sp.dma_start(e_w2[par], b.rearrange("a (f p) d -> p (a f) d", p=P)).then_inc(d_ew[par], 16)

            def load_bias(e, par):
                d = eb2[bass.ds(e, 1)] if not isinstance(e, int) else eb2[e:e + 1]
                sp.dma_start(e_b2[par], d.rearrange("a d -> (a d)").partition_broadcast(P)).then_inc(d_ew[par], 16)

            slot_tiles = slot_x.rearrange("(e r) d -> e r d", e=E)

            def load_rows(e, par):
                src = slot_tiles[e:e + 1] if isinstance(e, int) else slot_tiles[bass.ds(e, 1)]
                sp.dma_start(e_x[par][:, 0:FULL, :], src[:, 0:FULL * P, :].rearrange(
                    "a (i p) d -> p (a i) d", p=P)).then_inc(d_ex[par], 16)
                sp.dma_start(e_x[par][0:1, FULL, :], src[:, FULL * P:CAP, :].rearrange(
                    "a r d -> (a r) d")).then_inc(d_ex[par], 16)

            load_weights(0, 0)
            load_weights(1, 1)
            for k, places in enumerate(SCATTERS):
                sp.wait_ge(d_scatter[k], 16 * sum(map(len, places)))
            for e in range(2):
                load_rows(e, e)
                load_bias(e, e)
            with sp.Fori(0, (E - 2) // 2) as i:
                for k in range(2):
                    e = i * 2 + k
                    sp.wait_ge(e_rows_psum[1], e + 1)
                    load_rows(e + 2, k)
                    sp.wait_ge(e_y_ready[1], e + 1)
                    load_weights(e + 2, k)
                    load_bias(e + 2, k)

            for g in range(NG):
                if g < NG - GC:
                    sp.wait_ge(out_ready, g + 1)
                else:
                    sp.wait_ge(ffn_added, 1 + STEPS - NG + g + 1)
                sp.dma_start(out_dram[:, cols(g, GC), :], xin[:, cols(g, GC), :]).then_inc(d_out, 16)
            sp.wait_ge(d_out, 16 * NG)

        @block.tensor
        def _(pe):
            def transpose(dst, src, last=None):
                mm = pe.transpose(dst, src, ident[0:src.shape[0], 0:src.shape[0]])
                if last is not None:
                    mm.then_inc(last, 1)

            def mm(dst, lhsT, rhs, start=True, stop=True):
                return pe.matmul(dst, lhsT, rhs, start=start, stop=stop)

            pe.wait_ge(d_const, 16)
            for i in range(NG + 2):
                g = i
                if g < NG:
                    if g % 2 == 0:
                        pe.wait_ge(ln0_done, g // 2 + 1)
                    if g >= 2:
                        pe.wait_ge(g_xT_ready, g - 1)
                    for j in range(GC):
                        transpose(bank[g % 2][:, cols(j)], res[:, GC * g + j, :], g_xT_psum if j == GC - 1 else None)
                g = i - 1
                if 0 <= g < NG:
                    if g == 0:
                        pe.wait_ge(d_gate, 16)
                    pe.wait_ge(g_xT_ready, g + 1)
                    if g >= 2:
                        pe.wait_ge(g_lT_ready, g - 1)
                    mm(bank[2 + g % 2][0:E, :], gw_sb[:, :], xnT[g % 2]).then_inc(g_lT_psum, 1)
                g = i - 2
                if g >= 0:
                    pe.wait_ge(g_lT_ready, g + 1)
                    for j in range(GC):
                        c = GC * g + j
                        transpose(bank[4][:, cols(c, E)], lT[g % 2][:, cols(j)], g_logits if c == NCH - 1 else None)

            def expert(e, par, n):
                def rows(x, parity, k):
                    pe.wait_ge(d_ex[parity], k)
                    for i in range(GC):
                        transpose(bank[0][:, cols(i)], x[:, i, :], e_rows_psum[0] if i == GC - 1 else None)
                    transpose(bank[1][:, 0:P], x[:, GC, :])
                    mm(bank[1][:, P:P + 1], x[0:1, FULL, :], ones[0:1, 0:1]).then_inc(e_rows_psum[1], 1)

                first = isinstance(e, int) and e == 0
                final = isinstance(e, int) and e == E - 1
                half = (e >> 1) if not isinstance(e, int) else e // 2
                if first:
                    rows(e_x[0], 0, 32)
                pe.wait_ge(d_ew[par], (half + 1) * 48)
                for f in range(FB):
                    w = e_w1[par][:, cols(f)]
                    if f == 0:
                        pe.wait_ge(e_xT_ready[0], n(0))
                    need(pe, e_ha_ready[(f + 2) % FB], n(0) if f >= 2 else n(-1))
                    mm(bank[2 + f % 2][:, :], w, e_xT[par][:, 0:GT]).then_inc(e_ha_psum[f], 1)
                    if f == 0:
                        pe.wait_ge(e_xT_ready[1], n(0))
                    need(pe, e_hb_ready[(f + 2) % FB], n(0) if f >= 2 else n(-1))
                    mm(bank[4 + f % 2][:, 0:CAP - GT], w, e_xT[par][:, GT:CAP]).then_inc(e_hb_psum[f], 1)
                if not final:
                    rows(e_x[1 - par], 1 - par, (((e + 1) >> 1) + 1) * 32)
                need(pe, e_y_ready[0], n(-1))
                for i in range(FULL + 1):
                    m = P if i < FULL else TAIL
                    dst = bank[6][:, cols(i)] if i < GC else bank[7][0:m, cols(i - GC)]
                    if i == GC:
                        need(pe, e_y_ready[1], n(-1))
                    for f in range(FB):
                        if i == 0:
                            pe.wait_ge(e_ha_ready[f], n(0))
                        if i == GC:
                            pe.wait_ge(e_hb_ready[f], n(0))
                        last = mm(dst, e_hT[:, f, P * i:P * i + m], e_w2[par][:, f, :], f == 0, f == FB - 1)
                    if i == GC - 1:
                        last.then_inc(e_y_psum[0], 1)
                last.then_inc(e_y_psum[1], 1)

            def experts():
                t = EXPERTS_AT
                for s, k in ((probs_ready[GC - 1], t), (qkv_read[GC - 1], t + 1), (y_ready, t), (gate_ready, t + 1),
                             (kT_ready, t + 1), (q_ready, t + 1)):
                    pe.wait_ge(s, k)
                run_experts(pe, expert)
                for s in (e_y_ready[1], e_ha_ready[FB - 1], e_hb_ready[FB - 1]):
                    pe.wait_ge(s, E)

            def free(name, t, n):
                got = before(name, t)
                if got is not None:
                    need(pe, got[0], n(got[1] + (1 if got[0] is ffn_added else 0)))

            def project(t, n, j):
                need(pe, qkv_read[(j + 3) % GC], n(1) if j else n(0))
                if isinstance(t, int) and t == -1 and j == 0:
                    pe.wait_ge(v_centred, 1)
                mm(bank[2][:, 0:3 * P], xT[:, cols(j)], row(wqkv_all, layer_of(t + 1))).then_inc(qkv_psum[j], 1)

            halves = [slice(0, HP), slice(HP, P)]

            def scores(t, par, n, j):
                need_alone(pe, probs_ready[(j + 3) % GC], n(0) if j else n(-1))
                if j == 0:
                    if isinstance(t, int) and t == 0:
                        pe.wait_ge(g_slots, 1)
                    for s in (kT_ready, qa_ready, qb_ready):
                        need_alone(pe, s, n(0))
                for q in range(2):
                    for a in range(2):
                        c = slice(P * j + HP * a, P * j + HP * a + HP)
                        mm(bank[q][halves[a], 0:4 * HP], kT[halves[q], par, c], qT[halves[q], par, 0:4, c])
                for a in range(2):
                    for c in range(2):
                        last = mm(bank[a][halves[c], 4 * HP:4 * HP + HP],
                                  qk[halves[a], par, j, P + HP * c:P + HP * c + HP],
                                  padded_heads(vpad[halves[a], par, j, P * c:P * c + P]))
                last.then_inc(scores_psum[j], 1)

            def values(par, n, j):
                if j == 0:
                    need(pe, y_ready, n(-1))
                pe.wait_ge(smask_ready[j], n(0))
                for a in range(2):
                    for c in halves:
                        pe.matmul(bank[4 - a][c, cols(j, HP)], smask[:, (2 * j + a) % 4, c],
                                  qT[:, par, 4, P * j + HP * a:P * j + HP * a + HP],
                                  start=True, stop=False, skip_group_check=True)
                need_alone(pe, probs_ready[j], n(0))
                for h in range(H):
                    r = 32 * (h // 2)
                    for a in range(2):
                        last = pe.matmul(bank[4 - a][r:r + 32, cols(j, HP)], vpad[halves[a], par, j, cols(h, 32)],
                                         probs[halves[a], j % 2, h // 4, cols(h % 4, HP)], start=False,
                                         stop=h % 2 == 1, tile_position=(HP * a, r), skip_group_check=True)
                last.then_inc(av_done[j], 1)

            def ranks():
                pe.wait_ge(g_onehot, 1)
                mm(bank[0][:, 0:256], tri, gt["onehot"])
                mm(bank[1][:, 0:256], ones, gt["onehot"]).then_inc(g_ranks, 1)

            def transposes(name, src, done, width=P):
                for j in range(GC):
                    transpose(ring_bank(name)[:, cols(j, width)], src(j), done if j == GC - 1 else None)

            def step(t, par, n):
                s1, s2, s3, s4 = stages(t)
                if s2:
                    scores(t, par, n, 0)
                if s1:
                    free("t1", t, n)
                    pe.wait_ge(xhat_ready, n(1))
                    transposes("t1", lambda j: xhat[:, j, :], t1_psum)
                if s4:
                    free("wo", t, n)
                    pe.wait_ge(zT_ready, n(-2))
                    for j in range(GC):
                        last = mm(ring_bank("wo")[:, cols(j)], zT[:, cols(j)], row(wo_all, layer_of(t - 2)))
                    last.then_inc(wo_psum, 1)
                if s3:
                    free("var", t, n)
                    pe.wait_ge(y_ready, n(-1))
                    for j in range(GC):
                        for a in range(2):
                            last = mm(ring_bank("var")[halves[a], cols(j, H)], ysq[:, cols(2 * j + a, HP)], blockmean)
                    last.then_inc(var_psum, 1)
                if s1:
                    if isinstance(t, int) and t == -1:
                        pe.wait_ge(d_params, PARAMS)
                    pe.wait_ge(xT_ready, n(1))
                    project(t, n, 0)
                    if isinstance(t, int) and t == -1:
                        ranks()
                    free("g", t, n)
                    pe.wait_ge(wg_ready, n(1))
                    mm(ring_bank("g")[:, :], wg_now[:, :], xT[:, :]).then_inc(g_psum, 1)
                if s2:
                    scores(t, par, n, 1)
                    values(par, n, 0)
                if s1:
                    project(t, n, 1)
                if s2:
                    scores(t, par, n, 2)
                if s4:
                    free("t2", t, n)
                    pe.wait_ge(x2hat_ready, n(-2))
                    transposes("t2", lambda j: xhat2[:, j, :], t2_psum)
                if s2:
                    values(par, n, 1)
                if s4:
                    free("w1a", t, n)
                    pe.wait_ge(x2T_ready, n(-2))
                    pe.wait_ge(w1_ready, n(-2))
                    mm(ring_bank("w1a")[:, :], w1_now[:, 0:P], x2T[:, :]).then_inc(w1a_psum, 1)
                if s1:
                    project(t, n, 2)
                if s2:
                    scores(t, par, n, 3)
                if s4:
                    free("w1b", t, n)
                    mm(ring_bank("w1b")[:, :], w1_now[:, P:2 * P], x2T[:, :]).then_inc(w1b_psum, 1)
                if s1:
                    project(t, n, 3)
                if s2:
                    values(par, n, 2)
                if s3:
                    free("rt", t, n)
                    pe.wait_ge(rstdx_ready, n(-1))
                    transposes("rt", lambda j: rstdx[:, cols(j)], rt_psum)

                def second_product(chunks):
                    wl = row(w2_all, layer_of(t - 2))
                    for j in chunks:
                        for f in range(2):
                            last = mm(ring_bank("w2")[:, cols(j)], hT[:, f, cols(j)], wl[:, :, cols(f)],
                                      f == 0, f == 1)
                    return last

                if s4:
                    free("w2", t, n)
                    pe.wait_ge(ha_ready, n(-2))
                    pe.wait_ge(hb_ready, n(-2))
                    second_product((0, 1))
                if s1:
                    for j in range(GC):
                        pe.wait_ge(qk_ready[j], n(1))
                    free("tq", t, n)
                    transposes("tq", lambda j: qk[:, 1 - par, j, 0:P], tq_psum)
                    free("tk", t, n)
                    transposes("tk", lambda j: qk[:, 1 - par, j, P:2 * P], tk_psum)
                if s4:
                    second_product((2, 3)).then_inc(w2_psum, 1)
                if s2:
                    values(par, n, 3)

            run_steps(pe, step, experts)

        @block.scalar
        def _(act):
            act.dma_start(gw_sb[:, :], gate).then_inc(d_gate, 16)
            for dst, src in ((wqkv_all, wqkv), (wg_all, wg), (ln_sb, ln), (b1_sb, eb1), (gn_sb, gn), (wo_all, wo),
                             (w1_all, w1), (w2_all, w2)):
                act.dma_start(dst[:], src).then_inc(d_params, 16)
            for k in range(2):
                rows = cols(k, SCH // 2)
                act.dma_start(ropec[:, rows, :], rope_c[:, rows, :]).then_inc(d_rope[k], 16)
                act.dma_start(ropes[:, rows, :], rope_s[:, rows, :]).then_inc(d_rope[k], 16)

            for g in range(NG + 1):
                if g < NG:
                    act.wait_ge(g_xT_psum, g + 1)
                    act.copy(xnT[g % 2], bank[g % 2][:, :]).then_inc(g_xT_ready, 1)
                if g >= 1:
                    act.wait_ge(g_lT_psum, g)
                    act.copy(lT[(g - 1) % 2], bank[2 + (g - 1) % 2][0:E, :]).then_inc(g_lT_ready, 1)
            act.wait_ge(g_shifted, 1)
            act.activation(gt["exp"], gt["shifted"], ACT.Exp).then_inc(g_exp, 1)

            def expert(e, par, n):
                for f in range(FB):
                    b = row(b1_sb, e * FB + f)
                    need_alone(act, e_ha_psum[f], n(0))
                    act.activation(e_hT[:, f, 0:GT], bank[2 + f % 2][:, :], ACT.Gelu, bias=b).then_inc(e_ha_ready[f], 1)
                    need_alone(act, e_hb_psum[f], n(0))
                    act.activation(e_hT[:, f, GT:CAP], bank[4 + f % 2][:, 0:CAP - GT], ACT.Gelu,
                                   bias=b).then_inc(e_hb_ready[f], 1)

            def next_first(k, n):
                if not isinstance(k, int) or k + 2 < STEPS:
                    act.wait_ge(t1_psum, n(2))
                    act.activation(xT[:, :], ring_bank("t1")[:, :], ACT.Identity, bias=ln_sb[:, 1:2],
                                   scale=ln_sb[:, 0:1]).then_inc(xT_ready, 1)

            def experts():
                run_experts(act, expert)
                next_first(EXPERTS_AT - 1, Counts(act, EXPERTS_AT - 1))

            def as_row(ap):
                return ap.unsqueeze(1)

            act.wait_ge(d_params, PARAMS)
            act.copy(wg_now[:, :], wg_all[:, 0, :]).then_inc(wg_ready, 1)

            def step(t, par, n):
                s1, s2, s3, s4 = stages(t)
                if s1:
                    act.wait_ge(g_psum, n(1))
                    i = (t + 1) % 4 if isinstance(t, int) else (t + 1) & 3
                    act.activation(row(gateT, i), as_row(ring_bank("g")[:, :]), ACT.Silu).then_inc(gate_ready, 1)
                    if not isinstance(t, int) or t + 2 < STEPS:
                        act.copy(as_row(wg_now[:, :]), row(wg_all, layer_of(t + 2))).then_inc(wg_ready, 1)
                if s4:
                    act.wait_ge(t2_psum, n(-2))
                    act.activation(x2T[:, :], ring_bank("t2")[:, :], ACT.Identity, bias=ln_sb[:, 1:2],
                                   scale=ln_sb[:, 0:1]).then_inc(x2T_ready, 1)
                if s4:
                    act.wait_ge(w1a_psum, n(-2))
                    act.activation(hT[:, 0, :], ring_bank("w1a")[:, :], ACT.Gelu_apprx_tanh).then_inc(ha_ready, 1)
                if s3:
                    act.wait_ge(rstd_ready, n(-1))
                    act.copy(rstdx[:, :].rearrange("p (h d) -> p h d", d=DH),
                             rstd[:, :].unsqueeze(2).to_broadcast([P, GC * H, DH])).then_inc(rstdx_ready, 1)
                if s4:
                    act.wait_ge(w1b_psum, n(-2))
                    act.activation(hT[:, 1, :], ring_bank("w1b")[:, :], ACT.Gelu_apprx_tanh).then_inc(hb_ready, 1)
                if not isinstance(t, int) or 0 <= t - 1 < STEPS:
                    act.copy(as_row(w1_now[:, :]), row(w1_all, layer_of(t - 1))).then_inc(w1_ready, 1)
                if s1:
                    act.wait_ge(tq_psum, n(1))
                    act.copy(qT[:, 1 - par, 4, :], ring_bank("tq")[:, :]).then_inc(q_ready, 1)
                    act.wait_ge(tk_psum, n(1))
                    act.copy(kT[:, 1 - par, :], ring_bank("tk")[:, :]).then_inc(kT_ready, 1)
                    act.wait_ge(q_ready, n(1))
                    act.activation(qT[:, 1 - par, 0, :], qT[:, 1 - par, 4, :], ACT.Copy,
                                   scale=cst[:, HEADMASK:HEADMASK + 1]).then_inc(qa_ready, 1)
                if s2:
                    act.wait_ge(av_done[GC - 1], n(0))
                    need(act, zT_ready, n(-1))
                    for a in range(2):
                        src = bank[4 - a][:, 0:GC * HP].rearrange("p (j n) -> p j n", j=GC)
                        dst = slice(a, 2 * GC, 2)
                        act.copy(ysb[:, :].rearrange("p (j n) -> p j n", n=HP)[:, dst, :], src)
                        last = act.activation(ysq[:, :].rearrange("p (j n) -> p j n", n=HP)[:, dst, :], src, ACT.Square)
                    last.then_inc(y_ready, 1)
                if not isinstance(t, int) or t + 1 != EXPERTS_AT:
                    next_first(t, n)

            next_first(-2, Counts(act, -2))
            run_steps(act, step, experts)

        @block.vector
        def _(dve):
            links = [0]

            def link(ins):
                links[0] += 1
                ins.then_inc(chained, 1)
                dve.wait_ge(chained, links[0])

            def tt(out, a, b, op):
                return nc.vector.tensor_tensor(out, a, b, op)

            def apply0(k):
                dve.wait_ge(ln0_rstd, k + 1)
                for c in range(8 * k, 8 * k + 8):
                    last = nc.vector.tensor_scalar(res[:, c, :], xin[:, c, :], mv0[:, c, 0:1], rs0[:, c:c + 1],
                                                   ALU.subtract, ALU.mult)
                last.then_inc(ln0_done, 1)

            for k in range(4):
                dve.wait_ge(d_x[k], 16)
                for c in range(8):
                    last = nc.vector.bn_stats(stats[:, c, :], xin[:, 8 * k + c, :])
                link(last)
                for c in range(8):
                    last = nc.vector.bn_aggr(mv0[:, 8 * k + c, :], stats[:, c, :])
                link(last)
                nc.vector.tensor_scalar(ve0[:, cols(k, 8)], mv0[:, cols(k, 8), 1], EPS, None, ALU.add).then_inc(ln0_var, 1)
                if k > 0:
                    apply0(k - 1)
            apply0(3)

            def ln_apply(i, mv, rs, dst, done):
                x = group_rows(res, i)
                for j in range(GC):
                    last = nc.vector.tensor_scalar(dst[:, j, :], x[:, j, :], mv[:, j, 0:1], rs[:, j:j + 1],
                                                   ALU.subtract, ALU.mult)
                last.then_inc(done, 1)

            ln1 = (stats[:, 0:GC], mv1, ve1, ln1_st, ln1_mv, ln1_var)
            ln2 = (stats[:, GC:2 * GC], mv2, ve2, ln2_st, ln2_mv, ln2_var)

            def ln_stats(i, which, value):
                st, mv, ve, stat_done, mean_done, var_done = which
                x = group_rows(res, i)
                for j in range(GC):
                    last = nc.vector.bn_stats(st[:, j, :], x[:, j, :])
                last.then_inc(stat_done, 1)
                need_alone(dve, stat_done, value)
                for j in range(GC):
                    last = nc.vector.bn_aggr(mv[:, j, :], st[:, j, :])
                last.then_inc(mean_done, 1)
                dve.wait_ge(mean_done, value)
                nc.vector.tensor_scalar(ve[:, :], mv[:, :, 1], EPS, None, ALU.add).then_inc(var_done, 1)

            dve.wait_ge(ln0_done, 4)
            ln_stats(0, ln1, 1)
            dve.wait_ge(ln1_rstd, 1)
            ln_apply(0, mv1, rs1, xhat, xhat_ready)

            dve.wait_ge(d_params, PARAMS)
            wv = wqkv_all[:, :, 2 * P:3 * P].rearrange("p l (h d) -> p l h d", d=DH)
            mean = vare[:, :].rearrange("p (l h) -> p l h", l=L)
            link(nc.vector.tensor_reduce(mean, wv, AX.X, ALU.add))
            link(nc.vector.tensor_scalar(mean, mean, -1.0 / DH, None, ALU.mult))
            for l in range(L):
                last = tt(wv[:, l], wv[:, l], mean[:, l, :].unsqueeze(2).to_broadcast([P, H, DH]), ALU.add)
            last.then_inc(v_centred, 1)

            def by_chunk(ap):
                return ap.rearrange("p (c e) -> p c e", e=E)

            def by_expert(ap):
                return ap.rearrange("p (e c) -> p c e", e=E)

            def over_e(ap):
                return ap.unsqueeze(2).to_broadcast([P, NCH, E])

            revexp = cst[:, REVEXP:REVEXP + E].unsqueeze(1).to_broadcast([P, NCH, E])
            dve.wait_ge(g_logits, 1)
            logit = bank[4][:, 0:256]
            link(nc.vector.tensor_reduce(gsm["max"][:, :], by_chunk(logit), AX.X, ALU.max))
            tt(by_chunk(gt["shifted"]), by_chunk(logit), over_e(gsm["max"][:, :]), ALU.subtract).then_inc(g_shifted, 1)
            link(tt(by_chunk(gt["equal"]), by_chunk(logit), over_e(gsm["max"][:, :]), ALU.is_equal))
            link(tt(by_chunk(gt["score"]), by_chunk(gt["equal"]), revexp, ALU.mult))
            link(nc.vector.tensor_reduce(gsm["rev"][:, :], by_chunk(gt["score"]), AX.X, ALU.max))
            tt(by_expert(gt["onehot"]), revexp, over_e(gsm["rev"][:, :]), ALU.is_equal).then_inc(g_onehot, 1)
            dve.wait_ge(g_exp, 1)
            link(nc.vector.tensor_reduce(gsm["sum"][:, :], by_chunk(gt["exp"]), AX.X, ALU.add))
            link(nc.vector.reciprocal(gsm["inv"][:, :], gsm["sum"][:, :]))
            dve.wait_ge(g_ranks, 1)
            link(nc.vector.tensor_tensor_scan(gt["scan"], cst[:, NOTFIRST:NOTFIRST + 256], bank[1][:, 0:256], 0.0,
                                              ALU.mult, ALU.add))
            link(tt(gt["rank"], gt["scan"], bank[0][:, 0:256], ALU.add))
            link(tt(g_prod, gt["rank"], gt["onehot"], ALU.mult))
            link(nc.vector.tensor_reduce(gsm["rank"][:, :], by_expert(g_prod), AX.X, ALU.add))
            link(nc.vector.tensor_scalar(gsm["kept"][:, :], gsm["rank"][:, :], float(CAP), None, ALU.is_le))
            tt(weight[:, :], gsm["inv"][:, :], gsm["kept"][:, :], ALU.mult)
            nc.vector.tensor_scalar(gsm["far"][:, :], gsm["kept"][:, :], -1e6, 1e6, ALU.mult, ALU.add)
            link(nc.vector.scalar_tensor_tensor(out=gsm["slot"][:, :], in0=gsm["rev"][:, :], scalar=-float(CAP),
                                                in1=gsm["rank"][:, :], op0=ALU.mult, op1=ALU.add))
            nc.vector.scalar_tensor_tensor(out=slots[:, :], in0=gsm["slot"][:, :], scalar=float(E * CAP - 1),
                                           in1=gsm["far"][:, :], op0=ALU.add, op1=ALU.add).then_inc(g_slots, 1)

            nc.vector.memset(slot_now[:, :], 0).then_inc(merged, 1)
            nc.vector.memset(stats[:, 0, :], 0.0).then_inc(ffn_added, 1)
            nc.vector.memset(flat(state), 0.0).then_inc(state_zero, 1)
            dve.wait_ge(state_zero, 1)

            def expert(e, par, n):
                half = (e >> 1) if not isinstance(e, int) else e // 2
                def take(parity, k):
                    dve.wait_ge(e_rows_psum[0], k)
                    nc.vector.tensor_copy(e_xT[parity][:, 0:GT], bank[0][:, :]).then_inc(e_xT_ready[0], 1)
                    dve.wait_ge(e_rows_psum[1], k)
                    nc.vector.tensor_copy(e_xT[parity][:, GT:CAP], bank[1][:, 0:CAP - GT]).then_inc(e_xT_ready[1], 1)

                if isinstance(e, int) and e == 0:
                    take(0, 1)
                if not (isinstance(e, int) and e == E - 1):
                    take(1 - par, n(1))
                dve.wait_ge(d_ew[par], (half + 1) * 48)
                need(dve, d_ey[par], half * 32)
                dve.wait_ge(e_y_psum[0], n(0))
                tt(e_y[par][:, 0:GC, :], bank[6][:, :].rearrange("p (i d) -> p i d", d=D),
                   e_b2[par].unsqueeze(1).to_broadcast([P, GC, D]), ALU.add).then_inc(e_y_ready[0], 1)
                dve.wait_ge(e_y_psum[1], n(0))
                tt(e_y[par][:, GC, :], bank[7][:, 0:P], e_b2[par], ALU.add)
                tt(e_y[par][0:1, FULL, :], bank[7][0:1, P:2 * P], e_b2[par][0:1, :], ALU.add).then_inc(e_y_ready[1], 1)

            def experts():
                run_experts(dve, expert)

            def scores(t, n, j):
                need(dve, state_ready[(j + 3) % GC], n(0) if j else n(-1))
                need(dve, smask_ready[(j + 3) % GC], n(0) if j else n(-1))
                need(dve, av_done[(j + 2) % GC], n(0) if j >= 2 else n(-1))
                g = group_of(t) & (GC - 1)
                keep, deckeep = (row(cst, g + KEEP), row(cst, g + DECKEEP)) if j == 0 else (1.0, cst[:, DECAY:DECAY + 1])

                def masked(a, keep):
                    return nc.vector.scalar_tensor_tensor(
                        out=smask[:, (2 * j + a) % 4, :].rearrange("p (c v) -> p c v", c=2),
                        in0=state[:, a, :].unsqueeze(1).to_broadcast([P, 2, HP]), scalar=keep,
                        in1=blockdec.rearrange("p (c v) -> p c v", c=2), op0=ALU.mult, op1=ALU.mult)

                def with_half(a, decay):
                    return nc.vector.scalar_tensor_tensor(out=state[:, 1 - a, :], in0=state[:, a, :], scalar=decay,
                                                          in1=bank[a][:, 4 * HP:5 * HP], op0=ALU.mult, op1=ALU.add)

                def causal_scores(q):
                    return tt(probs[:, j % 2, q, :].rearrange("p (v n) -> p v n", v=4),
                              bank[q][:, 0:4 * HP].rearrange("p (v n) -> p v n", v=4),
                              causal.unsqueeze(1).to_broadcast([P, 4, HP]), ALU.mult)

                masked(0, keep)
                dve.wait_ge(scores_psum[j], n(0))
                with_half(0, deckeep).then_inc(half_ready[j], 1)
                causal_scores(0)
                dve.wait_ge(half_ready[j], n(0))
                with_half(1, cst[:, DECAY:DECAY + 1]).then_inc(state_ready[j], 1)
                causal_scores(1).then_inc(probs_ready[j], 1)
                masked(1, 1.0).then_inc(smask_ready[j], 1)

            def rotate(t, par, n, j):
                if isinstance(t, int) and t in (-1, 1) and j == 0:
                    dve.wait_ge(d_rope[(t + 1) // 2], 32)
                if isinstance(t, int) and t == -1 and j == 0:
                    dve.wait_ge(cleared, 2)
                dve.wait_ge(qkv_psum[j], n(1))
                nc.vector.tensor_copy(padded_heads(vpad[:, 1 - par, j, :]),
                                      bank[2][:, 2 * P:3 * P].rearrange("p (r w d) -> p r w d", r=4, w=2))
                need(dve, qk_ready[(j + 2) % GC], n(1) if j >= 2 else n(0))
                src = bank[2][:, 0:2 * P].unsqueeze(1)
                tt(rc[:, j % 2:j % 2 + 1, :], src, chunk_row(ropec, t + 1, j), ALU.mult)

                def pairs(ap):
                    return ap.rearrange("p a (h s d) -> p (a h) s d", s=2, d=DH // 2)

                tt(pairs(rs_[:, j % 2:j % 2 + 1, :]), pairs(src)[:, :, ::-1, :],
                   pairs(chunk_row(ropes, t + 1, j)), ALU.mult).then_inc(qkv_read[j], 1)
                if isinstance(t, int) and t < EXPERTS_AT:
                    dve.wait_ge(qkv_read[j], n(1))
                    tt(qk[:, 1 - par, j, :], rc[:, j % 2, :], rs_[:, j % 2, :], ALU.add).then_inc(qk_ready[j], 1)

            def merge(c, rows):
                nc.vector.scalar_tensor_tensor(out=row(xin, c), in0=rows, scalar=row(weight, c), in1=row(xin, c),
                                               op0=ALU.mult, op1=ALU.add).then_inc(merged, 1)

            def plus_res(g):
                dve.wait_ge(merged, 1 + GC * (g + 1))
                x = xin[:, cols(g, GC), :]
                return tt(x, x, res[:, cols(g, GC), :], ALU.add)

            def step(t, par, n):
                s1, s2, s3, s4 = stages(t)
                s0 = not isinstance(t, int) or t + 2 < STEPS
                if s2:
                    scores(t, n, 0)
                if s4:
                    dve.wait_ge(wo_psum, n(-2))
                    x = group_rows(res, t - 2)
                    tt(x, x, ring_bank("wo")[:, :].rearrange("p (j d) -> p j d", d=D), ALU.add).then_inc(attn_added, 1)
                    need_alone(dve, attn_added, n(-2))
                    ln_stats(t - 2, ln2, n(-2))
                if s1:
                    rotate(t, par, n, 0)
                if s3:
                    dve.wait_ge(var_psum, n(-1))
                    nc.vector.tensor_scalar(vare[:, :], ring_bank("var")[:, 0:GC * H], EPS, None,
                                            ALU.add).then_inc(vare_ready, 1)
                if s2:
                    scores(t, n, 1)
                if s4:
                    dve.wait_ge(ln2_rstd, n(-2))
                    ln_apply(t - 2, mv2, rs2, xhat2, x2hat_ready)
                if isinstance(t, int) and t == STEPS:
                    dve.wait_ge(d_gather_last, 16 * routed.shape[1])
                    for c in range(LAST + 1 - FIRST, NCH):
                        merge(c, row(routed, c - (LAST + 1 - FIRST)))
                    for g in range(NG - GC):
                        plus_res(g).then_inc(out_ready, 1)
                if s1:
                    rotate(t, par, n, 1)
                if s2:
                    scores(t, n, 2)
                if s0:
                    ln_stats(t + 2, ln1, n(2))
                if s1:
                    rotate(t, par, n, 2)
                if s2:
                    scores(t, n, 3)
                if s1:
                    rotate(t, par, n, 3)
                if s0:
                    dve.wait_ge(ln1_rstd, n(2))
                    need(dve, t1_psum, n(1))
                    ln_apply(t + 2, mv1, rs1, xhat, xhat_ready)
                if s3:
                    dve.wait_ge(rt_psum, n(-1))
                    l = layer_of(t - 1)
                    nc.vector.scalar_tensor_tensor(out=ysb[:, :], in0=ring_bank("rt")[:, :], scalar=row(gn_sb, l),
                                                   in1=ysb[:, :], op0=ALU.mult, op1=ALU.mult).then_inc(z1_ready, 1)
                    dve.wait_ge(z1_ready, n(-1))
                    i = (t - 1) % 4 if isinstance(t, int) else (t - 1) & 3
                    nc.vector.scalar_tensor_tensor(out=zT[:, :].unsqueeze(1), in0=ysb[:, :].unsqueeze(1),
                                                   scalar=row(gn_sb, l + L), in1=row(gateT, i), op0=ALU.add,
                                                   op1=ALU.mult).then_inc(zT_ready, 1)
                if s1:
                    dve.wait_ge(q_ready, n(1))
                    for v in range(1, 4):
                        last = nc.vector.tensor_scalar(qT[:, 1 - par, v, :], qT[:, 1 - par, 4, :],
                                                       cst[:, HEADMASK + v:HEADMASK + v + 1], None, ALU.mult)
                    last.then_inc(qb_ready, 1)
                if s4:
                    x = group_rows(res, t - 2)
                    if isinstance(t, int) and t - 2 >= STEPS - GC:
                        x = group_rows(xin, t - 2)
                        plus_res(group_of(t - 2)).then_inc(summed, 1)
                        dve.wait_ge(summed, t - 1 - (STEPS - GC))
                    dve.wait_ge(w2_psum, n(-2))
                    tt(x, x, ring_bank("w2")[:, :].rearrange("p (j d) -> p j d", d=D), ALU.add).then_inc(ffn_added, 1)
                if not isinstance(t, int):
                    need_alone(dve, d_gather, t * 16 - 16 * (FIRST - 1))
                    merge(t - FIRST, rows_now[:, :, :])

            run_steps(dve, step, experts)

        @block.gpsimd
        def _(pool):
            nc.gpsimd.memset(zeros, 0.0).then_inc(zeroed, 1)
            nc.gpsimd.memset(power[:, :], -0.5).then_inc(cleared, 1)
            nc.gpsimd.memset(vpad[:].rearrange("p a b c -> p (a b c)"), 0.0).then_inc(cleared, 1)
            pool.wait_ge(cleared, 2)

            def reciprocal_root(out, v):
                return nc.gpsimd.tensor_tensor(out, v, power[:, 0:v.shape[1]], ALU.pow)

            for k in range(4):
                pool.wait_ge(ln0_var, k + 1)
                reciprocal_root(rs0[:, cols(k, 8)], ve0[:, cols(k, 8)]).then_inc(ln0_rstd, 1)

            pool.wait_ge(ln1_var, 1)
            reciprocal_root(rs1[:, :], ve1[:, :]).then_inc(ln1_rstd, 1)

            def scatter(t, place):
                if not isinstance(t, int) or t + 1 >= len(SCATTERS):
                    return
                if t == -1 and place == 1:
                    pool.wait_ge(g_slots, 1)
                    pool.wait_ge(ln0_done, 4)
                    pool.wait_ge(d_zero, 16 * (E * D // P))
                for c in SCATTERS[t + 1][place]:
                    nc.gpsimd.indirect_dma_start(
                        out=slot_x, out_offset=bass.IndirectOffsetOnAxis(ap=slots[:, c:c + 1], axis=0),
                        in_=res[:, c, :], in_offset=None, bounds_check=E * CAP - 1,
                        oob_is_err=False).then_inc(d_scatter[t + 1], 16)

            def gather(rows, offsets, done):
                nc.gpsimd.indirect_dma_start(
                    out=rows, out_offset=None, in_=slot_y,
                    in_offset=bass.IndirectOffsetOnAxis(ap=offsets, axis=0),
                    bounds_check=E * CAP - 1, oob_is_err=False).then_inc(done, 16)

            slot_tiles = slot_y.rearrange("(e r) d -> e r d", e=E)

            def expert(e, par, n):
                dst = slot_tiles[e:e + 1] if isinstance(e, int) else slot_tiles[bass.ds(e, 1)]
                pool.wait_ge(e_y_ready[1], n(0))
                pool.dma_start(dst[:, 0:FULL * P, :].rearrange("a (i p) d -> p (a i) d", p=P),
                               e_y[par][:, 0:FULL, :]).then_inc(d_ey[par], 16)
                pool.dma_start(dst[:, FULL * P:CAP, :].rearrange("a r d -> (a r) d"),
                               e_y[par][0:1, FULL, :]).then_inc(d_ey[par], 16)

            def experts():
                run_experts(pool, expert)
                for k in range(2):
                    pool.wait_ge(d_ey[k], 32 * (E // 2))

            def rotated(t, par, n, j):
                if isinstance(t, int) and t < EXPERTS_AT:
                    return
                pool.wait_ge(qkv_read[j], n(1))
                nc.gpsimd.tensor_tensor(qk[:, 1 - par, j, :], rc[:, j % 2, :], rs_[:, j % 2, :],
                                        ALU.add).then_inc(qk_ready[j], 1)

            def step(t, par, n):
                s1, s2, s3, s4 = stages(t)
                scatter(t, 0)
                if s4:
                    pool.wait_ge(ln2_var, n(-2))
                    reciprocal_root(rs2[:, :], ve2[:, :]).then_inc(ln2_rstd, 1)
                if s1:
                    rotated(t, par, n, 0)
                if s3:
                    pool.wait_ge(vare_ready, n(-1))
                    reciprocal_root(rstd[:, :], vare[:, :]).then_inc(rstd_ready, 1)
                if s1:
                    rotated(t, par, n, 1)
                scatter(t, 1)
                if s1:
                    rotated(t, par, n, 2)
                if not isinstance(t, int) or t + 2 < STEPS:
                    pool.wait_ge(ln1_var, n(2))
                    reciprocal_root(rs1[:, :], ve1[:, :]).then_inc(ln1_rstd, 1)
                scatter(t, 2)
                if s1:
                    rotated(t, par, n, 3)
                if not isinstance(t, int):
                    need_alone(pool, merged, t + (1 - FIRST))
                    nc.gpsimd.memset(rows_now[:, 0, :], 0.0).then_inc(slot_ready, 1)
                    nc.gpsimd.tensor_copy(slot_now[:, :], row(slots, t - FIRST)).then_inc(slot_ready, 1)
                    need_alone(pool, slot_ready, t * 2 - 2 * (FIRST - 1))
                    gather(rows_now[:, 0, :], slot_now[:, :], d_gather)
                if isinstance(t, int) and t == LAST + 1:
                    nc.gpsimd.memset(flat(routed), 0.0).then_inc(cleared, 1)
                    pool.wait_ge(cleared, 3)
                    for k in range(routed.shape[1]):
                        gather(routed[:, k, :], slots[:, LAST + 1 - FIRST + k:LAST + 2 - FIRST + k], d_gather_last)
                scatter(t, 3)

            run_steps(pool, step, experts)


def kernel(**inputs):
    import concourse.bacc as _bacc
    from concourse.bass_utils import run_bass_kernel_spmd as _run

    a = {k: np.asarray(v) for k, v in inputs.items()}
    B, S, D = a["L0_attn_X"].shape
    H, DH = 8, 16
    order = np.arange(D).reshape(H, DH // 2, 2).transpose(0, 2, 1).reshape(D)
    qkv = [a["L0_attn_Wq"][:, :, order], a["L0_attn_Wk"][:, :, order], a["L0_attn_Wv"]]
    L, F = a["L0_attn_W1"].shape[0], a["L0_attn_W1"].shape[2]
    consts, rope_c, rope_s = shape_constants(S, H, DH)
    arrays = {
        "x": a["L0_attn_X"].reshape(B * S, D),
        "wqkv": np.concatenate(qkv, axis=2).transpose(1, 0, 2),
        "wg": a["L0_attn_Wg"].transpose(1, 0, 2),
        "wo": a["L0_attn_Wo"].transpose(1, 0, 2),
        "w1": a["L0_attn_W1"].transpose(1, 0, 2),
        "w2": a["L0_attn_W2"].reshape(L, F // P, P, D).transpose(2, 0, 1, 3).reshape(P, L, (F // P) * D),
        "ln": np.stack([a["L0_attn_ln_scale"], a["L0_attn_ln_bias"]], axis=1),
        "gn": np.concatenate([a["L0_attn_gn_scale"], a["L0_attn_gn_bias"]], axis=0).T,
        "gate": a["L0_ffn_wg"],
        "ew1": a["L0_ffn_W1"],
        "eb1": a["L0_ffn_b1"].reshape(a["L0_ffn_b1"].shape[0], -1, P).transpose(2, 0, 1).reshape(P, -1),
        "ew2": a["L0_ffn_W2"],
        "eb2": a["L0_ffn_b2"],
        "consts": consts,
        "rope_c": rope_c,
        "rope_s": rope_s,
    }
    arrays = {f"in_{k}": np.ascontiguousarray(v) for k, v in arrays.items()}
    nc = _bacc.Bacc("TRN2", target_bir_lowering=False, num_devices=1)
    args = [nc.dram_tensor(k, v.shape, mybir.dt.from_np(v.dtype), kind="ExternalInput").ap() for k, v in arrays.items()]
    args.append(nc.dram_tensor("out_0", (B * S, D), F32, kind="ExternalOutput").ap())
    retention_moe(nc, *args)
    r = _run(nc, [arrays], core_ids=[0])
    return r.results[0]["out_0"].reshape(B, S, D)
```
